# Optimizing a Trainium2 kernel written in Bass

```python
import numpy as np
import jax
import jax.numpy as jnp

def _softmax(x, axis=-1):
    return jax.nn.softmax(x, axis=axis)

def _gelu(x):
    return jax.nn.gelu(x, approximate=True)

def _silu(x):
    return jax.nn.silu(x)

def _sigmoid(x):
    return jax.nn.sigmoid(x)

def _layernorm(x, axis=-1, eps=1e-05):
    m = jnp.mean(x, axis=axis, keepdims=True)
    v = jnp.var(x, axis=axis, keepdims=True)
    return (x - m) / jnp.sqrt(v + eps)

def _scatter_add(tgt, idx, src, axis=0):
    return tgt.at[idx].add(src)

def _segment_sum(src, seg, n):
    return jax.ops.segment_sum(src, seg, n)
kernel_name = 'mk_vit_tower_d1_tok_img1024_r4_df9e49'

def setup_inputs(seed: int=0):
    np.random.seed(seed)
    _w = jnp.asarray

    def _rec_inputs():
        import jax
        import jax.numpy as jnp
        _rk = jax.random.key(seed)
        x = -0.000356955 + 1 * jax.random.normal(jax.random.fold_in(_rk, 1), (64, 3, 224, 224), jnp.float32)
        return x
    x = _rec_inputs()

    def _L0_tok_setup():
        import jax, jax.numpy as jnp
        import numpy as np
        PATCH = 16
        EMBED = 256
        key = jax.random.key(seed)
        kx, kw = jax.random.split(key, 2)
        x = jax.random.normal(kx, (128, 3, 224, 224), dtype=jnp.float32)
        in_feat = PATCH * PATCH * 3
        W = jax.random.normal(kw, (EMBED, in_feat), dtype=jnp.float32) * 0.02
        b = jnp.zeros((EMBED,), dtype=jnp.float32)
        return {'x': x, 'W': W, 'b': b}
    _L0_tok_all = _L0_tok_setup()
    _L0_tok_in = {k: v for k, v in _L0_tok_all.items() if k in ('W', 'b')}
    del _L0_tok_all

    def _L0_attn_setup():
        import jax, jax.numpy as jnp
        import numpy as np
        INPUT_SIZE = 256
        STATE_SIZE = 256
        OUTPUT_SIZE = 256
        key = jax.random.key(seed)
        ks = jax.random.split(key, 8)
        B, T = (8, 512)
        u = jax.random.normal(ks[0], (B, T, INPUT_SIZE), dtype=jnp.float32)
        log_A = jax.random.normal(ks[1], (STATE_SIZE,), dtype=jnp.float32) * 0.5
        sB = 1.0 / np.sqrt(INPUT_SIZE)
        sC = 1.0 / np.sqrt(STATE_SIZE)
        sD = 1.0 / np.sqrt(INPUT_SIZE)
        W_B = jax.random.uniform(ks[2], (STATE_SIZE, INPUT_SIZE), jnp.float32, -sB, sB)
        b_B = jax.random.uniform(ks[3], (STATE_SIZE,), jnp.float32, -sB, sB)
        W_C = jax.random.uniform(ks[4], (OUTPUT_SIZE, STATE_SIZE), jnp.float32, -sC, sC)
        b_C = jax.random.uniform(ks[5], (OUTPUT_SIZE,), jnp.float32, -sC, sC)
        W_D = jax.random.uniform(ks[6], (OUTPUT_SIZE, INPUT_SIZE), jnp.float32, -sD, sD)
        b_D = jax.random.uniform(ks[7], (OUTPUT_SIZE,), jnp.float32, -sD, sD)
        log_dt = jnp.full((1,), -1.0, dtype=jnp.float32)
        return {'u': u, 'log_A': log_A, 'W_B': W_B, 'b_B': b_B, 'W_C': W_C, 'b_C': b_C, 'W_D': W_D, 'b_D': b_D, 'log_dt': log_dt}
    _L0_attn_all = _L0_attn_setup()
    _L0_attn_in = {k: v for k, v in _L0_attn_all.items() if k in ('log_A', 'W_B', 'b_B', 'W_C', 'b_C', 'W_D', 'b_D', 'log_dt')}
    del _L0_attn_all

    def _L0_ffn_setup():
        import jax, jax.numpy as jnp
        import numpy as np
        D = 256
        H = 4
        HD = D // H
        E = 8
        FF = 1024
        CAP_FACTOR = 1.0

        def _ln(x, g, b, eps=1e-05):
            mu = jnp.mean(x, -1, keepdims=True)
            v = jnp.mean((x - mu) ** 2, -1, keepdims=True)
            return (x - mu) * jax.lax.rsqrt(v + eps) * g + b

        def _mha(x, w, b, ow, ob):
            L, N, _ = x.shape
            qkv = x @ w.T + b
            q, k, v = jnp.split(qkv, 3, axis=-1)
            rh = lambda t: t.reshape(L, N, H, HD).transpose(1, 2, 0, 3)
            q, k, v = (rh(q), rh(k), rh(v))
            scores = jnp.einsum('nhld,nhmd->nhlm', q, k) / np.float32(np.sqrt(HD))
            attn = jax.nn.softmax(scores, axis=-1)
            o = jnp.einsum('nhlm,nhmd->nhld', attn, v).transpose(2, 0, 1, 3).reshape(L, N, D)
            return o @ ow.T + ob

        def _moe(x, wg, w1, b1, w2, b2):
            L, N, _ = x.shape
            S = L * N
            cap = int(CAP_FACTOR * S) // E
            xf = x.reshape(S, D)
            gates = jax.nn.softmax(xf @ wg, axis=-1)
            idx = jnp.argmax(gates, axis=-1)
            mask1 = jax.nn.one_hot(idx, E, dtype=x.dtype)
            loc = jnp.sum((jnp.cumsum(mask1, 0) - 1.0) * mask1, -1).astype(jnp.int32)
            keep = loc < cap
            gate_val = jnp.take_along_axis(gates, idx[:, None], -1)[:, 0]
            slot = jnp.where(keep, idx.astype(jnp.int32) * cap + loc, E * cap)
            disp = jnp.zeros((E * cap, D), x.dtype).at[slot].set(xf, mode='drop')
            disp = disp.reshape(E, cap, D)
            h = jnp.einsum('ecd,edf->ecf', disp, w1) + b1[:, None, :]
            y = (jnp.einsum('ecf,efd->ecd', h, w2) + b2[:, None, :]).reshape(E * cap, D)
            out = jnp.where(keep[:, None], gate_val[:, None] * y[jnp.minimum(slot, E * cap - 1)], 0.0)
            return out.reshape(L, N, D)
        key = jax.random.key(seed)
        ks = jax.random.split(key, 8)
        L, N = (256, 16)
        s = 0.02
        return {'x': jax.random.normal(ks[0], (L, N, D), jnp.float32), 'in_proj_w': jax.random.normal(ks[1], (3 * D, D), jnp.float32) * s, 'in_proj_b': jnp.zeros((3 * D,), jnp.float32), 'out_proj_w': jax.random.normal(ks[2], (D, D), jnp.float32) * s, 'out_proj_b': jnp.zeros((D,), jnp.float32), 'ln1_g': jnp.ones((D,), jnp.float32), 'ln1_b': jnp.zeros((D,), jnp.float32), 'ln2_g': jnp.ones((D,), jnp.float32), 'ln2_b': jnp.zeros((D,), jnp.float32), 'wg': jax.random.normal(ks[3], (D, E), jnp.float32) * s, 'w1': jax.random.normal(ks[4], (E, D, FF), jnp.float32) * s, 'b1': jnp.zeros((E, FF), jnp.float32), 'w2': jax.random.normal(ks[5], (E, FF, D), jnp.float32) * s, 'b2': jnp.zeros((E, D), jnp.float32)}
    _L0_ffn_all = _L0_ffn_setup()
    _L0_ffn_in = {k: v for k, v in _L0_ffn_all.items() if k in ('in_proj_w', 'in_proj_b', 'out_proj_w', 'out_proj_b', 'ln1_g', 'ln1_b', 'ln2_g', 'ln2_b', 'wg', 'w1', 'b1', 'w2', 'b2')}
    del _L0_ffn_all
    return {'x': x, 'L0_tok_W': _L0_tok_in['W'], 'L0_tok_b': _L0_tok_in['b'], 'L0_attn_log_A': _L0_attn_in['log_A'], 'L0_attn_W_B': _L0_attn_in['W_B'], 'L0_attn_b_B': _L0_attn_in['b_B'], 'L0_attn_W_C': _L0_attn_in['W_C'], 'L0_attn_b_C': _L0_attn_in['b_C'], 'L0_attn_W_D': _L0_attn_in['W_D'], 'L0_attn_b_D': _L0_attn_in['b_D'], 'L0_attn_log_dt': _L0_attn_in['log_dt'], 'L0_ffn_in_proj_w': _L0_ffn_in['in_proj_w'], 'L0_ffn_in_proj_b': _L0_ffn_in['in_proj_b'], 'L0_ffn_out_proj_w': _L0_ffn_in['out_proj_w'], 'L0_ffn_out_proj_b': _L0_ffn_in['out_proj_b'], 'L0_ffn_ln1_g': _L0_ffn_in['ln1_g'], 'L0_ffn_ln1_b': _L0_ffn_in['ln1_b'], 'L0_ffn_ln2_g': _L0_ffn_in['ln2_g'], 'L0_ffn_ln2_b': _L0_ffn_in['ln2_b'], 'L0_ffn_wg': _L0_ffn_in['wg'], 'L0_ffn_w1': _L0_ffn_in['w1'], 'L0_ffn_b1': _L0_ffn_in['b1'], 'L0_ffn_w2': _L0_ffn_in['w2'], 'L0_ffn_b2': _L0_ffn_in['b2']}

def reference(x, L0_tok_W, L0_tok_b, L0_attn_log_A, L0_attn_W_B, L0_attn_b_B, L0_attn_W_C, L0_attn_b_C, L0_attn_W_D, L0_attn_b_D, L0_attn_log_dt, L0_ffn_in_proj_w, L0_ffn_in_proj_b, L0_ffn_out_proj_w, L0_ffn_out_proj_b, L0_ffn_ln1_g, L0_ffn_ln1_b, L0_ffn_ln2_g, L0_ffn_ln2_b, L0_ffn_wg, L0_ffn_w1, L0_ffn_b1, L0_ffn_w2, L0_ffn_b2):
    import jax
    import jax.numpy as jnp

    def _L0_tok_ref(x, W, b):
        import jax, jax.numpy as jnp
        import numpy as np
        PATCH = 16
        EMBED = 256
        p = PATCH
        B, C, H, Wd = x.shape
        gh, gw = (H // p, Wd // p)
        patches = x.reshape(B, C, gh, p, gw, p).transpose(0, 1, 2, 4, 3, 5)
        patches = patches.reshape(B, gh * gw, p * p * C)
        return jnp.einsum('bnk,ek->bne', patches, W) + b

    def _L0_attn_ref(u, log_A, W_B, b_B, W_C, b_C, W_D, b_D, log_dt):
        import jax, jax.numpy as jnp
        import numpy as np
        INPUT_SIZE = 256
        STATE_SIZE = 256
        OUTPUT_SIZE = 256
        dt = jnp.exp(log_dt)
        A = -jnp.exp(log_A)
        A_bar = jnp.exp(A * dt)
        Bu = (jnp.einsum('bti,ni->btn', u, W_B) + b_B) * dt
        Bu_t = jnp.swapaxes(Bu, 0, 1)

        def step(x, bu):
            x = A_bar * x + bu
            return (x, x)
        x0 = jnp.zeros((u.shape[0], A_bar.shape[0]), dtype=u.dtype)
        _, xs = jax.lax.scan(step, x0, Bu_t)
        xs = jnp.swapaxes(xs, 0, 1)
        y = jnp.einsum('btn,on->bto', xs, W_C) + b_C + jnp.einsum('bti,oi->bto', u, W_D) + b_D
        return y

    def _L0_ffn_ref(x, in_proj_w, in_proj_b, out_proj_w, out_proj_b, ln1_g, ln1_b, ln2_g, ln2_b, wg, w1, b1, w2, b2):
        import jax, jax.numpy as jnp
        import numpy as np
        D = 256
        H = 4
        HD = D // H
        E = 8
        FF = 1024
        CAP_FACTOR = 1.0

        def _ln(x, g, b, eps=1e-05):
            mu = jnp.mean(x, -1, keepdims=True)
            v = jnp.mean((x - mu) ** 2, -1, keepdims=True)
            return (x - mu) * jax.lax.rsqrt(v + eps) * g + b

        def _mha(x, w, b, ow, ob):
            L, N, _ = x.shape
            qkv = x @ w.T + b
            q, k, v = jnp.split(qkv, 3, axis=-1)
            rh = lambda t: t.reshape(L, N, H, HD).transpose(1, 2, 0, 3)
            q, k, v = (rh(q), rh(k), rh(v))
            scores = jnp.einsum('nhld,nhmd->nhlm', q, k) / np.float32(np.sqrt(HD))
            attn = jax.nn.softmax(scores, axis=-1)
            o = jnp.einsum('nhlm,nhmd->nhld', attn, v).transpose(2, 0, 1, 3).reshape(L, N, D)
            return o @ ow.T + ob

        def _moe(x, wg, w1, b1, w2, b2):
            L, N, _ = x.shape
            S = L * N
            cap = int(CAP_FACTOR * S) // E
            xf = x.reshape(S, D)
            gates = jax.nn.softmax(xf @ wg, axis=-1)
            idx = jnp.argmax(gates, axis=-1)
            mask1 = jax.nn.one_hot(idx, E, dtype=x.dtype)
            loc = jnp.sum((jnp.cumsum(mask1, 0) - 1.0) * mask1, -1).astype(jnp.int32)
            keep = loc < cap
            gate_val = jnp.take_along_axis(gates, idx[:, None], -1)[:, 0]
            slot = jnp.where(keep, idx.astype(jnp.int32) * cap + loc, E * cap)
            disp = jnp.zeros((E * cap, D), x.dtype).at[slot].set(xf, mode='drop')
            disp = disp.reshape(E, cap, D)
            h = jnp.einsum('ecd,edf->ecf', disp, w1) + b1[:, None, :]
            y = (jnp.einsum('ecf,efd->ecd', h, w2) + b2[:, None, :]).reshape(E * cap, D)
            out = jnp.where(keep[:, None], gate_val[:, None] * y[jnp.minimum(slot, E * cap - 1)], 0.0)
            return out.reshape(L, N, D)
        y1 = _ln(x + _mha(x, in_proj_w, in_proj_b, out_proj_w, out_proj_b), ln1_g, ln1_b)
        y2 = _ln(y1 + _moe(y1, wg, w1, b1, w2, b2), ln2_g, ln2_b)
        return y2
    h = _L0_tok_ref(x, L0_tok_W, L0_tok_b)
    h = h + _L0_attn_ref(_layernorm(h, axis=-1), L0_attn_log_A, L0_attn_W_B, L0_attn_b_B, L0_attn_W_C, L0_attn_b_C, L0_attn_W_D, L0_attn_b_D, L0_attn_log_dt)
    h = h + _L0_ffn_ref(_layernorm(h, axis=-1), L0_ffn_in_proj_w, L0_ffn_in_proj_b, L0_ffn_out_proj_w, L0_ffn_out_proj_b, L0_ffn_ln1_g, L0_ffn_ln1_b, L0_ffn_ln2_g, L0_ffn_ln2_b, L0_ffn_wg, L0_ffn_w1, L0_ffn_b1, L0_ffn_w2, L0_ffn_b2)
    return h

_drawn_inputs = setup_inputs


def setup_inputs(seed=0):
    import zlib

    import numpy as np

    out = dict(_drawn_inputs(seed))
    spreads = {'L0_tok_b': (0.0, 0.1),
     'L0_ffn_in_proj_b': (0.0, 0.442),
     'L0_ffn_out_proj_b': (0.0, 0.1),
     'L0_ffn_ln1_g': (1.0, 0.2),
     'L0_ffn_ln1_b': (0.0, 0.1),
     'L0_ffn_ln2_g': (1.0, 0.2),
     'L0_ffn_ln2_b': (0.0, 0.1),
     'L0_ffn_b1': (0.0, 0.8),
     'L0_ffn_b2': (0.0, 0.8)}
    factors = {'L0_ffn_in_proj_w': 4.024, 'L0_ffn_w1': 2.816, 'L0_ffn_w2': 2.695}
    for name, (base, spread) in spreads.items():
        noise = np.random.default_rng([zlib.crc32(name.encode()), seed]).standard_normal(out[name].shape)
        drawn = base * np.exp(spread * noise) if base else spread * noise
        out[name] = jnp.asarray(drawn.astype(out[name].dtype))
    for name, factor in factors.items():
        out[name] = (out[name] * factor).astype(out[name].dtype)
    return out
```

```python
import concourse.bass as bass
from concourse import mybir
from contextlib import ExitStack

F32 = mybir.dt.float32
F32R = mybir.dt.float32r
BF16 = mybir.dt.bfloat16
I32 = mybir.dt.int32
ALU = mybir.AluOpType
ACT = mybir.ActivationFunctionType
AX_X = mybir.AxisListType.X

P = 128
L, N = 64, 196
S = L * N
D = 256
FT = D // P
KP = 768
KT = KP // P
H, HD = 4, 64
HS = HD + 1
NE, FF = 8, 1024
FK = FF // P
CAP = S // NE
EPS = 1e-5
G = 2 * P
NG = S // G
BIN = S + P
BINS = NE * BIN
TILES = 4 * ((S // P + NE + 3) // 4)
ROW = 2 * D + 2
OFF_GATE, OFF_S = 2 * D, 2 * D + 1
FAR = float(2 * S)

W_TOK = 0
W_B = W_TOK + KT * D
W_C = W_B + FT * D
W_D = W_C + FT * D
W_QKV = W_D + FT * D
W_OUT = W_QKV + FT * 3 * D
WCOLS = W_OUT + FT * D


class At:

    def __init__(self, t, c, u=2):
        self.t, self.c, self.u = t, c, u

    def back(self, s):
        return At(self.t, self.c - s, self.u)

    def n(self):
        return self.c if isinstance(self.t, int) else self.t * self.u + self.c

    def slot(self, r):
        return self.c % r

    def turn(self, r):
        return self.c // r if isinstance(self.t, int) else self.t * (self.u // r) + self.c // r

    def valid(self, count):
        return not isinstance(self.t, int) or 0 <= self.c < count


def wait(eng, sem, value, most=None):
    if isinstance(value, int):
        if most is not None:
            value = min(value, most)
        if value <= 0:
            return
    eng.wait_ge(sem, value)


def apart(eng, passed):
    eng.sem_inc(passed, 1)


def run(eng, step, first, last, lo, hi, u=2):
    for c in range(first, lo):
        step(At(0, c, u))
    with eng.Fori(0, (hi - lo) // u) as t:
        for c in range(u):
            step(At(t, lo + c, u))
    for c in range(hi, last):
        step(At(0, c, u))


def build(nc, xt, w_tok, b_tok, log_a, w_b, b_b, w_c, b_c, w_d, b_d, log_dt, w_in, b_qk, b_v, w_o, b_o,
          g1, be1, g2, be2, wg, w1t, b1c, w2, b2c, out):
    h1_dram = nc.dram_tensor("h1_dram", (S, D), F32, kind="Internal").ap()
    bins = nc.dram_tensor("bins", (BINS + P, ROW), F32, kind="Internal").ap()
    with ExitStack() as ctx:
        def sb(name, shape, dt=F32, c=ctx):
            return c.enter_context(nc.sbuf_tensor(name, shape, dt))

        def sem(name):
            return ctx.enter_context(nc.semaphore(name))

        wh, wl = sb("wh", [P, WCOLS], F32R), sb("wl", [P, WCOLS], F32R)
        w12 = sb("w12", [P, NE, FT * D])
        b12 = sb("b12", [P, NE, D])
        rows_c = sb("rows_c", [P, 8, D])
        r_btok, r_bcd, r_bo, r_g1, r_be1, r_g2, r_be2, r_bd = (rows_c[:, i, :] for i in range(8))
        cols_c = sb("cols_c", [P, 16])
        c_loga, c_bb, c_bqk, c_bv, c_dt = (cols_c[:, a:b] for a, b in ((0, 2), (2, 4), (4, 8), (8, 10), (10, 11)))
        c_a, c_bbdt = cols_c[:, 11:13], cols_c[:, 13:15]
        ident = sb("ident", [P, P])
        decay = sb("decay", [P, FT, G + N])
        wg_sb = sb("wg_sb", [P, FT, NE])
        mhalf = sb("mhalf", [P, 2])
        before = sb("before", [P, P], BF16)
        ones_b = sb("ones_b", [P, P], BF16)
        later_l = sb("later_l", [P, P])
        same_l = sb("same_l", [P, P])
        first_n = sb("first_n", [P, P])
        ebase = sb("ebase", [P, NE])
        rank8 = sb("rank8", [P, NE])
        s_tab = sb("s_tab", [P, 2 * NG])
        oh_all = sb("oh_all", [P, 2 * NG, NE], BF16)
        oh_acc = sb("oh_acc", [P, NE], BF16)
        fill = sb("fill", [P, ROW])

        with ExitStack() as pre:
            wf = sb("wf", [P, WCOLS], F32, pre)
            colf = sb("colf", [P, P], F32, pre)
            coli = sb("coli", [P, P], I32, pre)
            parti = sb("parti", [P, 2], I32, pre)
            partf = sb("partf", [P, 4], F32, pre)
            lcoli = sb("lcoli", [P, P], I32, pre)
            lcolf = sb("lcolf", [P, P], F32, pre)
            tmp8 = sb("tmp8", [P, NE], I32, pre)
            tmpe = sb("tmpe", [P, NE], I32, pre)
            stabi = sb("stabi", [P, 2 * NG], I32, pre)
            bvb = sb("bvb", [P, FT, P], F32, pre)
            ps_bo = pre.enter_context(nc.psum_tensor("ps_bo", [P, D], F32))
            passed = {e: sem("passed_" + e) for e in ("pool", "dve", "pe")}
            w_in_sem, c_in_sem = sem("w_loaded"), sem("consts_loaded")
            hi_done, pre_iota, own, act_own = sem("w_hi_done"), sem("iota_done"), sem("pre_dve"), sem("pre_act")
            bo_ready, bo_done, dt_col = sem("bv_spread"), sem("bo_product"), sem("dt_done")
            a_arg = sem("decay_arg")
            blk = pre.enter_context(nc.Block())

            @blk.sync
            def _(sp):
                for off, src in ((W_TOK, w_tok), (W_B, w_b), (W_C, w_c), (W_D, w_d), (W_QKV, w_in), (W_OUT, w_o)):
                    width = src.shape[1]
                    sp.dma_start(wf[:, off:off + width], src).then_inc(w_in_sem, 16)

            @blk.scalar
            def _(act):
                n = 0
                for dst, src in ((c_loga, log_a), (c_bb, b_b), (c_bqk, b_qk), (c_bv, b_v),
                                 (wg_sb[:].rearrange("p t e -> p (t e)"), wg)):
                    act.dma_start(dst, src).then_inc(c_in_sem, 16)
                for dst, src in ((r_btok, b_tok), (r_bcd, b_c), (r_bd, b_d), (r_bo, b_o), (r_g1, g1), (r_be1, be1),
                                 (r_g2, g2), (r_be2, be2), (c_dt, log_dt)):
                    act.dma_start(dst, src.partition_broadcast(P)).then_inc(c_in_sem, 16)
                act.wait_ge(c_in_sem, 14 * 16)
                nc.scalar.activation(c_dt, c_dt, ACT.Exp).then_inc(dt_col, 1)
                nc.scalar.activation(c_a, c_loga, ACT.Exp).then_inc(dt_col, 1)
                act.wait_ge(a_arg, 1)
                nc.scalar.activation(c_a, c_a, ACT.Exp).then_inc(act_own, 1)
                act.wait_ge(w_in_sem, 6 * 16)
                nc.scalar.activation(wh[:], wf[:], ACT.Copy).then_inc(hi_done, 1)

            @blk.gpsimd
            def _(pool):
                nc.gpsimd.iota(coli[:], [[1, P]], base=0, channel_multiplier=0).then_inc(pre_iota, 1)
                nc.gpsimd.iota(lcoli[:], [[0, 2], [1, L]], base=0, channel_multiplier=0).then_inc(pre_iota, 1)
                nc.gpsimd.iota(parti[:, 0:1], [[1, 1]], base=0, channel_multiplier=1).then_inc(pre_iota, 1)
                nc.gpsimd.iota(tmp8[:], [[-1, NE]], base=NE, channel_multiplier=0).then_inc(pre_iota, 1)
                nc.gpsimd.iota(tmpe[:], [[BIN, NE]], base=0, channel_multiplier=0).then_inc(pre_iota, 1)
                nc.gpsimd.iota(stabi[:], [[2, 2 * NG]], base=0, channel_multiplier=N).then_inc(pre_iota, 1)

            @blk.tensor
            def _(pe):
                pe.wait_ge(bo_ready, 1)
                pe.wait_ge(w_in_sem, 6 * 16)
                for t in range(FT):
                    last = nc.tensor.matmul(ps_bo[:], bvb[:, t, :], wf[:, W_OUT + t * D:W_OUT + (t + 1) * D],
                                            start=(t == 0), stop=(t == FT - 1))
                last.then_inc(bo_done, 1)

            @blk.vector
            def _(dve):
                v = nc.vector
                count = [0]

                def link(ins):
                    count[0] += 1
                    ins.then_inc(own, 1)
                    dve.wait_ge(own, count[0])

                v.memset(mhalf[:], -0.5)
                v.memset(ones_b[:], 1.0)
                v.memset(oh_acc[:], 0.0)
                v.memset(fill[:, 0:OFF_S], 0.0)
                v.memset(fill[:, OFF_S:ROW], FAR)
                dve.wait_ge(pre_iota, 6)
                link(v.tensor_copy(colf[:], coli[:]))
                link(v.tensor_copy(lcolf[:], lcoli[:]))
                link(v.tensor_copy(partf[:, 0:1], parti[:, 0:1]))
                v.tensor_copy(rank8[:], tmp8[:])
                v.tensor_copy(ebase[:], tmpe[:])
                link(v.tensor_copy(s_tab[:], stabi[:]))
                link(v.tensor_scalar(partf[:, 1:2], partf[:, 0:1], float(L), None, ALU.is_ge))
                link(v.scalar_tensor_tensor(partf[:, 2:3], partf[:, 1:2], -float(L), partf[:, 0:1], ALU.mult, ALU.add))
                v.tensor_scalar(ident[:], colf[:], partf[:, 0:1], None, ALU.is_equal)
                v.tensor_scalar(before[:], colf[:], partf[:, 0:1], None, ALU.is_gt)
                v.tensor_scalar(later_l[:], lcolf[:], partf[:, 2:3], None, ALU.is_gt)
                link(v.tensor_scalar(same_l[:], lcolf[:], partf[:, 2:3], None, ALU.is_equal))
                link(v.tensor_scalar(partf[:, 3:4], partf[:, 1:2], 1.0 - float(L * N), None, ALU.mult))
                link(v.tensor_scalar(s_tab[:], s_tab[:], partf[:, 3:4], None, ALU.add))
                link(v.tensor_scalar(partf[:, 3:4], partf[:, 1:2], -1.0, 1.0, ALU.mult, ALU.add))
                link(v.tensor_scalar(colf[:], colf[:], float(L), None, ALU.is_ge))
                link(v.tensor_scalar(first_n[:], colf[:], partf[:, 3:4], None, ALU.mult))
                link(v.tensor_tensor(first_n[:], first_n[:], same_l[:], ALU.mult))
                dve.wait_ge(c_in_sem, 14 * 16)
                link(v.tensor_tensor(r_bcd, r_bcd, r_bd, ALU.add))
                link(v.tensor_copy(bvb[:], c_bv.unsqueeze(2).to_broadcast([P, FT, P])))
                v.engine_nop().then_inc(bo_ready, 1)
                dve.wait_ge(dt_col, 2)
                v.tensor_scalar(c_bbdt, c_bb, c_dt, None, ALU.mult)
                v.tensor_scalar(c_a, c_a, c_dt, -1.0, ALU.mult, ALU.mult).then_inc(a_arg, 1)
                dve.wait_ge(act_own, 1)
                link(v.tensor_copy(decay[:], c_a.unsqueeze(2).to_broadcast([P, FT, G + N])))
                link(v.memset(decay[:, :, 0:G + N:N], 0.0))
                dve.wait_ge(bo_done, 1)
                link(v.tensor_tensor(r_bo, r_bo, ps_bo[:], ALU.add))
                dve.wait_ge(hi_done, 1)
                link(v.tensor_tensor(wl[:], wf[:], wh[:].bitcast(F32), ALU.subtract))

        def product(out_ps, pairs):
            terms = [(a, b) for (ah, al), (bh, bl) in pairs for a, b in ((ah, bh), (ah, bl), (al, bh))]
            for i, (a, b) in enumerate(terms):
                last = nc.tensor.matmul(out_ps, a, b, start=(i == 0), stop=(i == len(terms) - 1))
            return last

        def both(a, b, *idx):
            return a[idx], b[idx]

        with ExitStack() as pa:
            def pb(name, shape):
                return pa.enter_context(nc.psum_tensor(name, shape, F32))

            xf = sb("xf", [P, 2, KT * G], F32, pa)
            xh, xl = sb("xh", [P, 2, KT * G], F32R, pa), sb("xl", [P, 2, KT * G], F32R, pa)
            h = sb("h", [P, 2, 2, D], F32, pa)
            hb = sb("hb", [P, 2, 2, D], F32, pa)
            u = sb("u", [P, 2, 2, D], F32, pa)
            uh, ul = sb("uh", [P, 2, FT * G], F32R, pa), sb("ul", [P, 2, FT * G], F32R, pa)
            bu = sb("bu", [P, 2, FT, G], F32, pa)
            xs = sb("xs", [P, 2, FT, G], F32, pa)
            sh, sl = sb("sh", [P, 2, FT * G], F32R, pa), sb("sl", [P, 2, FT * G], F32R, pa)
            h1o = sb("h1o", [P, 2, 2, D], F32, pa)
            stats = sb("stats_a", [P, 2, 6], F32, pa)
            mv = sb("mv_a", [P, 2, 2], F32, pa)
            ve = sb("ve_a", [P, 2], F32, pa)
            rstd = sb("rstd_a", [P, 2], F32, pa)
            w1s = sb("w1s", [P, 1, FK * D], F32, pa)
            w2s = sb("w2s", [P, 1, FK * D], F32, pa)
            b1s = sb("b1s", [P, NE * FK], F32, pa)
            b2s = sb("b2s", [P, NE * FT], F32, pa)
            b12c = sb("b12c", [P, NE * FT, P], F32, pa)
            b12t = sb("b12t", [P, NE * FT], F32, pa)
            ps_h = [pb(f"ps_h{i}", [P, 2 * D]) for i in range(2)]
            ps_t = pb("ps_t", [P, FT * G])
            ps_b = pb("ps_b", [P, FT * G])
            ps_y = [pb(f"ps_y{i}", [P, 2 * D]) for i in range(2)]
            ps_f = pb("ps_f", [P, FT * D])
            ps_fb = pb("ps_fb", [P, 2 * D])

            x_loaded = [sem(f"x_loaded{i}") for i in range(2)]
            h1_stored = [sem(f"h1_stored{i}") for i in range(2)]
            (x_hi, x_lo, tok_done, h_done, st_done, mv_done, rstd_done, u_done, ut_done, u_hi, u_lo, bu_ps, bu_done,
             scan_done, s_hi, s_lo, y_done, hb_done, h1_done) = (sem("a_" + s) for s in (
                 "x_hi", "x_lo", "tok_done", "h_done", "stats_done", "meanvar_done", "rstd_done", "u_done",
                 "uT_done", "u_hi", "u_lo", "bu_ps", "bu_done", "scan_done", "s_hi", "s_lo", "y_done", "hb_done",
                 "h1_done"))
            wf_loaded, fold_ps, fold_out, fb_ps, fb_out = (sem(s) for s in (
                "fold_w_loaded", "fold_ps", "fold_out", "fold_bias_ps", "fold_bias_out"))
            fb_spread, fb_in, ve_done = sem("fold_bias_spread"), sem("fold_bias_loaded"), sem("a_eps_added")
            A_STEPS = (0, NG + 3, 6, 48)
            blk = pa.enter_context(nc.Block())
            h1_grp = h1_dram.rearrange("(g s p) d -> g p s d", s=2, p=P)

            @blk.sync
            def _(sp):
                def load(m):
                    wait(sp, x_hi, m.n() - 1)
                    wait(sp, x_lo, m.n() - 1)
                    sp.dma_start(xf[:, m.slot(2), :], xt[m.n()]).then_inc(x_loaded[m.slot(2)], 16)

                def store(m):
                    wait(sp, h1_done, m.n() + 1)
                    sp.dma_start(h1_grp[m.n()], h1o[:, m.slot(2)]).then_inc(h1_stored[m.slot(2)], 16)

                load(At(0, 0))
                load(At(0, 1))
                sp.dma_start(b1s[:], b1c).then_inc(fb_in, 16)
                sp.dma_start(b2s[:], b2c).then_inc(fb_in, 16)

                def step(k):
                    if k.back(-2).valid(NG):
                        load(k.back(-2))
                    if k.back(3).valid(NG):
                        store(k.back(3))

                run(sp, step, 0, NG + 3, 6, 46)
                for e in range(NE):
                    wait(sp, fold_ps, e)
                    sp.dma_start(w1s[:, 0, :], w1t[e]).then_inc(wf_loaded, 16)
                    sp.dma_start(w2s[:, 0, :], w2[e]).then_inc(wf_loaded, 16)
                for i in range(2):
                    sp.wait_ge(h1_stored[i], 16 * ((NG + 1 - i) // 2))

            @blk.scalar
            def _(act):
                def split_x(m):
                    p = m.slot(2)
                    wait(act, x_loaded[p], (m.turn(2) + 1) * 16)
                    wait(act, tok_done, m.n() - 1)
                    nc.scalar.activation(xh[:, p, :], xf[:, p, :], ACT.Copy).then_inc(x_hi, 1)

                def split_u(m):
                    wait(act, ut_done, m.n() + 1)
                    wait(act, y_done, m.n() - 1)
                    nc.scalar.activation(uh[:, m.slot(2), :], ps_t[:], ACT.Copy).then_inc(u_hi, 1)

                def inputs(m):
                    wait(act, bu_ps, m.n() + 1)
                    wait(act, scan_done, m.n() * 2 - 2)
                    for t in range(FT):
                        nc.scalar.activation(bu[:, m.slot(2), t, :], ps_b[:, t * G:(t + 1) * G], ACT.Identity,
                                             bias=c_bbdt[:, t:t + 1], scale=c_dt).then_inc(bu_done, 1)

                def split_s(m):
                    wait(act, scan_done, m.n() * 2 + 2)
                    wait(act, y_done, m.n() - 1)
                    nc.scalar.activation(sh[:, m.slot(2), :], xs[:, m.slot(2)].rearrange("p t g -> p (t g)"),
                                         ACT.Copy).then_inc(s_hi, 1)

                split_x(At(0, 0))

                def step(k):
                    for m, stage in ((k.back(1), split_u), (k.back(-1), split_x), (k.back(1), inputs),
                                     (k.back(1), split_s)):
                        if m.valid(NG):
                            stage(m)

                run(act, step, 0, NG + 3, 6, 48)
                for e in range(NE):
                    act.wait_ge(fold_ps, e + 1)
                    nc.scalar.activation(w12[:, e, :], ps_f[:], ACT.Copy).then_inc(fold_out, 1)

            @blk.gpsimd
            def _(pool):
                def norm(m):
                    wait(pool, mv_done, m.n() * 2 + 2)
                    apart(pool, passed["pool"])
                    nc.gpsimd.tensor_scalar(ve[:], mv[:, :, 1], EPS, None, ALU.add).then_inc(ve_done, 1)
                    wait(pool, ve_done, m.n() + 1)
                    nc.gpsimd.tensor_tensor(rstd[:], ve[:], mhalf[:], ALU.pow).then_inc(rstd_done, 1)

                def add_bias(m):
                    p = m.slot(2)
                    wait(pool, h_done, m.n() + 1)
                    wait(pool, h1_done, m.n() - 1)
                    nc.gpsimd.tensor_tensor(hb[:, p], h[:, p], r_bcd.unsqueeze(1).to_broadcast([P, 2, D]),
                                            ALU.add).then_inc(hb_done, 1)

                def step(k):
                    if k.valid(NG):
                        norm(k)
                        add_bias(k)

                run(pool, step, 0, NG, 6, 48)

            @blk.vector
            def _(dve):
                v = nc.vector

                def split_x(m):
                    p = m.slot(2)
                    wait(dve, x_hi, m.n() + 1)
                    wait(dve, tok_done, m.n() - 1)
                    v.tensor_tensor(xl[:, p, :], xf[:, p, :], xh[:, p, :].bitcast(F32), ALU.subtract).then_inc(x_lo, 1)

                def split_u(m):
                    p = m.slot(2)
                    wait(dve, u_hi, m.n() + 1)
                    wait(dve, y_done, m.n() - 1)
                    v.tensor_tensor(ul[:, p, :], ps_t[:], uh[:, p, :].bitcast(F32), ALU.subtract).then_inc(u_lo, 1)

                def scan(m):
                    p = m.slot(2)
                    wait(dve, bu_done, m.n() * 2 + 2)
                    wait(dve, s_hi, m.n() - 1)
                    wait(dve, scan_done, m.n() * 2)
                    first = isinstance(m.t, int) and m.c == 0
                    at = m.n() * G % N
                    for t in range(FT):
                        v.tensor_tensor_scan(xs[:, p, t, :], decay[:, t, bass.ds(at, G)], bu[:, p, t, :],
                                             0.0 if first else xs[:, 1 - p, t, G - 1:G],
                                             ALU.mult, ALU.add).then_inc(scan_done, 1)

                def split_s(m):
                    p = m.slot(2)
                    wait(dve, s_hi, m.n() + 1)
                    wait(dve, y_done, m.n() - 1)
                    v.tensor_tensor(sl[:, p, :], xs[:, p].rearrange("p t g -> p (t g)"), sh[:, p, :].bitcast(F32),
                                    ALU.subtract).then_inc(s_lo, 1)

                def hidden(m):
                    p = m.slot(2)
                    wait(dve, tok_done, m.n() + 1)
                    wait(dve, hb_done, m.n() - 1)
                    v.tensor_tensor(h[:, p], ps_h[p][:].rearrange("p (s d) -> p s d", s=2),
                                    r_btok.unsqueeze(1).to_broadcast([P, 2, D]), ALU.add).then_inc(h_done, 1)
                    wait(dve, h_done, m.n() + 1)
                    for s in range(2):
                        v.bn_stats(stats[:, s, :], h[:, p, s, :]).then_inc(st_done, 1)
                    wait(dve, st_done, m.n() * 2 + 2)
                    apart(dve, passed["dve"])
                    for s in range(2):
                        v.bn_aggr(mv[:, s, :], stats[:, s, :]).then_inc(mv_done, 1)
                    wait(dve, rstd_done, m.n() + 1)
                    wait(dve, ut_done, m.n() - 1)
                    for s in range(2):
                        v.tensor_scalar(u[:, p, s, :], h[:, p, s, :], mv[:, s, 0:1], rstd[:, s:s + 1],
                                        ALU.subtract, ALU.mult).then_inc(u_done, 1)

                def residual(m):
                    p = m.slot(2)
                    wait(dve, y_done, m.n() + 1)
                    wait(dve, hb_done, m.n() + 1)
                    wait(dve, h1_stored[p], m.turn(2) * 16)
                    v.tensor_tensor(h1o[:, p], ps_y[p][:].rearrange("p (s d) -> p s d", s=2), hb[:, p],
                                    ALU.add).then_inc(h1_done, 1)

                split_x(At(0, 0))

                def step(k):
                    for m, stage in ((k.back(1), split_u), (k.back(3), residual), (k.back(-1), split_x),
                                     (k.back(1), scan), (k.back(1), split_s), (k, hidden)):
                        if m.valid(NG):
                            stage(m)

                run(dve, step, 0, NG + 3, 6, 48)
                dve.wait_ge(fold_ps, NE)
                dve.wait_ge(fb_in, 32)
                v.tensor_tensor(b12t[:], ps_fb[:, 0:NE * FT], b2s[:], ALU.add).then_inc(fb_out, 1)
                dve.wait_ge(fb_out, 1)
                v.tensor_copy(b12c[:], b12t[:].unsqueeze(2).to_broadcast([P, NE * FT, P])).then_inc(fb_spread, 1)
                for e in range(0, NE, 2):
                    dve.wait_ge(fb_ps, 1 + e // 2)
                    v.tensor_copy(b12[:, e:e + 2, :], ps_fb[:].rearrange("p (e d) -> p e d", e=2)).then_inc(fb_out, 1)

            @blk.tensor
            def _(pe):
                def tokens(m, s):
                    p = m.slot(2)
                    if s == 0:
                        wait(pe, x_lo, m.n() + 1)
                        wait(pe, h_done, m.n() - 1)
                    last = product(ps_h[p][:, s * D:(s + 1) * D],
                                   [(both(xh, xl, slice(None), p, slice(t * G + s * P, t * G + (s + 1) * P)),
                                     both(wh, wl, slice(None), slice(W_TOK + t * D, W_TOK + (t + 1) * D)))
                                    for t in range(KT)])
                    if s == 1:
                        last.then_inc(tok_done, 1)

                def turn_u(m):
                    p = m.slot(2)
                    wait(pe, u_done, m.n() * 2 + 2)
                    wait(pe, u_lo, m.n())
                    for s in range(2):
                        for t in range(FT):
                            last = nc.tensor.transpose(ps_t[:, t * G + s * P:t * G + (s + 1) * P],
                                                       u[:, p, s, t * P:(t + 1) * P], ident[:])
                    last.then_inc(ut_done, 1)

                def inputs(m):
                    p = m.slot(2)
                    wait(pe, u_lo, m.n() + 1)
                    wait(pe, bu_done, m.n() * 2)
                    for o in range(FT):
                        last = product(ps_b[:, o * G:(o + 1) * G],
                                       [(both(wh, wl, slice(None), slice(W_B + t * D + o * P, W_B + t * D + (o + 1) * P)),
                                         both(uh, ul, slice(None), p, slice(t * G, (t + 1) * G))) for t in range(FT)])
                    last.then_inc(bu_ps, 1)

                def outputs(m):
                    p = m.slot(2)
                    wait(pe, s_lo, m.n() + 1)
                    wait(pe, h1_done, m.n() - 1)
                    for s in range(2):
                        last = product(ps_y[p][:, s * D:(s + 1) * D],
                                       [(both(a, b, slice(None), p, slice(t * G + s * P, t * G + (s + 1) * P)),
                                         both(wh, wl, slice(None), slice(w + t * D, w + (t + 1) * D)))
                                        for a, b, w in ((uh, ul, W_D), (sh, sl, W_C)) for t in range(FT)])
                    last.then_inc(y_done, 1)

                def step(k):
                    if k.valid(NG):
                        tokens(k, 0)
                    if k.back(1).valid(NG):
                        inputs(k.back(1))
                    if k.valid(NG):
                        tokens(k, 1)
                    if k.back(2).valid(NG):
                        outputs(k.back(2))
                    if k.valid(NG):
                        turn_u(k)

                run(pe, step, 0, NG + 2, 6, 48)
                for e in range(NE):
                    pe.wait_ge(wf_loaded, 32 * (e + 1))
                    if e == 0:
                        pe.wait_ge(fb_in, 32)
                    wait(pe, fold_out, e)
                    for c in range(FT):
                        for f in range(FK):
                            nc.tensor.matmul(ps_fb[:, e * FT + c:e * FT + c + 1], w2s[:, 0, f * D + c * P:f * D + (c + 1) * P],
                                             b1s[:, e * FK + f:e * FK + f + 1], start=(f == 0), stop=(f == FK - 1))
                    for c in range(FT):
                        for f in range(FK):
                            last = nc.tensor.matmul(ps_f[:, c * D:(c + 1) * D], w1s[:, 0, f * D + c * P:f * D + (c + 1) * P],
                                                    w2s[:, 0, f * D:(f + 1) * D], start=(f == 0), stop=(f == FK - 1))
                    last.then_inc(fold_ps, 1)
                pe.wait_ge(fb_spread, 1)
                for e in range(NE):
                    if e % 2 == 0:
                        pe.wait_ge(fb_out, 1 + e // 2)
                    for c in range(FT):
                        last = nc.tensor.matmul(ps_fb[:, (e % 2) * D + c * P:(e % 2) * D + (c + 1) * P],
                                                b12c[:, e * FT + c, :], ident[:], start=True, stop=True)
                    if e % 2:
                        last.then_inc(fb_ps, 1)

        with ExitStack() as pb_:
            def pb(name, shape):
                return pb_.enter_context(nc.psum_tensor(name, shape, F32))

            hin = sb("hin", [P, 2, 2, D], F32, pb_)
            x2 = sb("x2", [P, 2, 2, D], F32, pb_)
            x2b = sb("x2b", [P, 2, 2, D], F32, pb_)
            xh, xl = sb("x2h", [P, FT * G], F32R, pb_), sb("x2l", [P, FT * G], F32R, pb_)
            q, kk = sb("q", [P, FT * G], F32, pb_), sb("k", [P, FT * G], F32, pb_)
            va = sb("va", [P, 2, 2, H, HS], F32, pb_)
            ss = sb("ss", [P, 2, H, L], F32, pb_)
            eb = sb("eb", [P, 2, H, P], F32, pb_)
            et = sb("et", [P, 2, H * P], F32, pb_)
            o = sb("o", [P, 2, H, HD], F32, pb_)
            oh_, ol_ = sb("oTh", [P, FT * G], F32R, pb_), sb("oTl", [P, FT * G], F32R, pb_)
            z = sb("z", [P, 2, D], F32, pb_)
            zg = sb("zg", [P, 2, D], F32, pb_)
            y1t = sb("y1t", [P, FT * G], F32, pb_)
            rows = sb("rows", [P, 2, 2, ROW], F32, pb_)
            mx = sb("mx", [P, 2, 2, 2], F32, pb_)
            rinv = sb("rinv", [P, 2, H], F32, pb_)
            small = sb("small", [P, 16], F32, pb_)
            lmax, esum, cmax, slot_f = (small[:, i:i + 2] for i in (0, 2, 4, 6))
            slot_i = sb("slot_i", [P, 2, 2], I32, pb_)
            dl, el, cand, pos = (sb(s, [P, 2, NE], F32, pb_) for s in ("dl", "el", "cand", "pos"))
            oh = sb("oh", [P, 2, NE], BF16, pb_)
            st_x, st_z = sb("st_x", [P, 2, 6], F32, pb_), sb("st_z", [P, 2, 6], F32, pb_)
            mv_x, mv_z = sb("mv_x", [P, 2, 2], F32, pb_), sb("mv_z", [P, 2, 2], F32, pb_)
            ve_x, ve_z, rs_x, rs_z = (sb(s, [P, 2], F32, pb_) for s in ("ve_x", "ve_z", "rs_x", "rs_z"))
            b_0, b_1, b_3 = (pb(f"b_{i}", [P, 512]) for i in (0, 1, 3))
            ps_s = pb("ps_s", [P, 2, 512])
            ps_o = pb("ps_o", [P, 2, 512])
            b_2 = ps_o[:, 1, :]
            ps_r = pb("ps_r", [P, 512])
            logit = ps_r[:, 0:2 * NE].rearrange("p (s e) -> p s e", s=2)
            order = ps_r[:, 256:256 + 2 * NE].rearrange("p (s e) -> p s e", s=2)

            h_loaded = [sem(f"b_h_loaded{i}") for i in range(2)]
            r_loaded = [sem(f"b_row_loaded{i}") for i in range(2)]
            scattered = [sem(f"b_scattered{i}") for i in range(2)]
            names = ("xst xmv xve xrs x2 x2b x2T x2hi x2lo v_ps v_out q_ps q_out k_ps k_out s_ps max sub exp et_ps "
                     "et_out0 et_out1 av_ps rinv o oT o_hi o_lo out_ps z zst zmv zve zrs zg y1 y1T_ps y1T logit_ps lmax "
                     "dlog elog esum gate cand cmax onehot acc order_ps pos posm slot slot_i ohcopy scopy ones").split()
            Q = {s: sem("b_" + s) for s in names}
            h1_tok = h1_dram.rearrange("(l j s t) d -> t j l s d", l=L, j=NG, s=2, t=2)
            blk = pb_.enter_context(nc.Block())

            @blk.sync
            def _(sp):
                def load(m):
                    p = m.slot(2)
                    wait(sp, Q["x2"], m.n() * 2 - 2)
                    for t in range(2):
                        sp.dma_start(hin[t * L:(t + 1) * L, p], h1_tok[t, m.n()]).then_inc(h_loaded[p], 16)

                def load_row(m):
                    p = m.slot(2)
                    wait(sp, scattered[p], m.turn(2) * 32)
                    for t in range(2):
                        sp.dma_start(rows[t * L:(t + 1) * L, p, :, D:2 * D], h1_tok[t, m.n()]).then_inc(r_loaded[p], 16)

                load(At(0, 0))
                load(At(0, 1))

                def step(k):
                    if k.back(-2).valid(NG):
                        load(k.back(-2))
                    if k.back(2).valid(NG):
                        load_row(k.back(2))

                run(sp, step, 0, NG + 2, 6, 46)

            @blk.scalar
            def _(act):
                A = nc.scalar.activation

                def o_hi(m):
                    wait(act, Q["oT"], m.n() + 1)
                    wait(act, Q["out_ps"], m.n())
                    A(oh_[:], b_1[:], ACT.Copy).then_inc(Q["o_hi"], 1)

                def exps(m):
                    wait(act, Q["sub"], m.n() * 2 + 2)
                    wait(act, Q["et_ps"], m.n() * 2)
                    if isinstance(m.t, int):
                        act.wait_ge(Q["ones"], 2)
                    for t in range(2):
                        r = slice(t * L, (t + 1) * L)
                        A(eb[r, :, :, t * L:(t + 1) * L].rearrange("p s h m -> p (s h) m"),
                          ss[r].rearrange("p s h m -> p (s h) m"), ACT.Exp,
                          scale=1.0 / float(HD) ** 0.5).then_inc(Q["exp"], 1)

                def v_out(m):
                    wait(act, Q["v_ps"], m.n() + 1)
                    wait(act, Q["av_ps"], m.n() - 1)
                    A(va[:, m.slot(2), :, :, 0:HD], b_3[:].rearrange("p (s h d) -> p s h d", s=2, h=H),
                      ACT.Copy).then_inc(Q["v_out"], 1)

                def qk_out(m, ps, dst, at, done):
                    wait(act, Q[ps], m.n() + 1)
                    src = b_1 if ps == "q_ps" else b_2
                    for t in range(FT):
                        A(dst[:, t * G:(t + 1) * G], src[:, t * G:(t + 1) * G], ACT.Identity,
                          bias=c_bqk[:, at + t:at + t + 1]).then_inc(Q[done], 1)

                def e_log(m):
                    wait(act, Q["dlog"], m.n() + 1)
                    A(el[:], dl[:], ACT.Exp).then_inc(Q["elog"], 1)

                def et_out(m):
                    wait(act, Q["et_ps"], m.n() * 2 + 1)
                    wait(act, Q["av_ps"], m.n())
                    A(et[:, 0, :], b_1[:], ACT.Copy).then_inc(Q["et_out0"], 1)

                def x_hi(m):
                    wait(act, Q["x2T"], m.n() + 1)
                    A(xh[:], b_2, ACT.Copy).then_inc(Q["x2hi"], 1)

                def y1t_out(m):
                    wait(act, Q["y1T_ps"], m.n() + 1)
                    wait(act, Q["logit_ps"], m.n())
                    A(y1t[:], b_0[:], ACT.Copy).then_inc(Q["y1T"], 1)

                def step(k):
                    for m, stage in ((k.back(2), o_hi), (k.back(1), exps), (k, v_out), (k.back(3), e_log),
                                     (k, lambda m: qk_out(m, "q_ps", q, 0, "q_out")),
                                     (k, lambda m: qk_out(m, "k_ps", kk, FT, "k_out")),
                                     (k.back(1), et_out), (k.back(-1), x_hi), (k.back(2), y1t_out)):
                        if m.valid(NG):
                            stage(m)

                run(act, step, -1, NG + 3, 6, 48)

            @blk.gpsimd
            def _(pool):
                g = nc.gpsimd
                g.memset(eb[:], 0.0).then_inc(Q["ones"], 1)
                g.memset(va[:], 1.0).then_inc(Q["ones"], 1)

                def rstd(m, mv_s, ve_s, rs_s, mv_, ve_, rs_):
                    wait(pool, Q[mv_s], m.n() * 2 + 2)
                    apart(pool, passed["pool"])
                    g.tensor_scalar(ve_[:], mv_[:, :, 1], EPS, None, ALU.add).then_inc(Q[ve_s], 1)
                    wait(pool, Q[ve_s], m.n() + 1)
                    g.tensor_tensor(rs_[:], ve_[:], mhalf[:], ALU.pow).then_inc(Q[rs_s], 1)

                def add_bias(m):
                    p = m.slot(2)
                    wait(pool, Q["x2"], m.n() * 2 + 2)
                    wait(pool, Q["z"], m.n() - 1)
                    g.tensor_tensor(x2b[:, p], x2[:, p], r_bo.unsqueeze(1).to_broadcast([P, 2, D]),
                                    ALU.add).then_inc(Q["x2b"], 1)

                def send(m):
                    p = m.slot(2)
                    wait(pool, Q["onehot"], m.n() + 1)
                    apart(pool, passed["pool"])
                    g.tensor_copy(oh_all[:, bass.ds(m.n() * 2, 2), :], oh[:]).then_inc(Q["ohcopy"], 1)
                    wait(pool, r_loaded[p], (m.turn(2) + 1) * 32)
                    apart(pool, passed["pool"])
                    g.tensor_copy(rows[:, p, :, OFF_S], s_tab[:, bass.ds(m.n() * 2, 2)]).then_inc(Q["scopy"], 1)
                    wait(pool, Q["slot"], m.n() + 1)
                    apart(pool, passed["pool"])
                    g.tensor_copy(slot_i[:, p, :], slot_f).then_inc(Q["slot_i"], 1)
                    wait(pool, Q["slot_i"], m.n() + 1)
                    wait(pool, Q["scopy"], m.n() + 1)
                    wait(pool, Q["gate"], m.n() + 1)
                    apart(pool, passed["pool"])
                    for s in range(2):
                        g.indirect_dma_start(bins, bass.IndirectOffsetOnAxis(ap=slot_i[:, p, s:s + 1], axis=0),
                                             rows[:, p, s, :], None).then_inc(scattered[p], 16)

                def step(k):
                    if k.back(-1).valid(NG):
                        rstd(k.back(-1), "xmv", "xve", "xrs", mv_x, ve_x, rs_x)
                    if k.valid(NG):
                        add_bias(k)
                    if k.back(2).valid(NG):
                        rstd(k.back(2), "zmv", "zve", "zrs", mv_z, ve_z, rs_z)
                    if k.back(3).valid(NG):
                        send(k.back(3))

                run(pool, step, -1, NG + 3, 6, 48)
                for i in range(2):
                    pool.wait_ge(scattered[i], 32 * ((NG + 1 - i) // 2))

            @blk.vector
            def _(dve):
                v = nc.vector

                def x_norm(m):
                    p = m.slot(2)
                    wait(dve, h_loaded[p], (m.turn(2) + 1) * 32)
                    for s in range(2):
                        v.bn_stats(st_x[:, s, :], hin[:, p, s, :]).then_inc(Q["xst"], 1)
                    wait(dve, Q["xst"], m.n() * 2 + 2)
                    apart(dve, passed["dve"])
                    for s in range(2):
                        v.bn_aggr(mv_x[:, s, :], st_x[:, s, :]).then_inc(Q["xmv"], 1)
                    wait(dve, Q["xrs"], m.n() + 1)
                    wait(dve, Q["x2T"], m.n() - 1)
                    wait(dve, Q["x2b"], m.n() - 1)
                    for s in range(2):
                        v.tensor_scalar(x2[:, p, s, :], hin[:, p, s, :], mv_x[:, s, 0:1], rs_x[:, s:s + 1],
                                        ALU.subtract, ALU.mult).then_inc(Q["x2"], 1)

                def x_lo(m):
                    wait(dve, Q["x2hi"], m.n() + 1)
                    v.tensor_tensor(xl[:], b_2, xh[:].bitcast(F32), ALU.subtract).then_inc(Q["x2lo"], 1)

                def o_lo(m):
                    wait(dve, Q["o_hi"], m.n() + 1)
                    wait(dve, Q["out_ps"], m.n())
                    v.tensor_tensor(ol_[:], b_1[:], oh_[:].bitcast(F32), ALU.subtract).then_inc(Q["o_lo"], 1)

                def softmax(m):
                    wait(dve, Q["s_ps"], m.n() + 1)
                    wait(dve, Q["exp"], m.n() * 2)
                    sv = [ps_s[:, :, s * 2 * L:(s + 1) * 2 * L].rearrange("p a (b m) -> p a b m", b=2) for s in range(2)]
                    for s in range(2):
                        v.tensor_reduce(mx[:, s], sv[s], AX_X, ALU.max).then_inc(Q["max"], 1)
                    wait(dve, Q["max"], m.n() * 2 + 2)
                    for s in range(2):
                        v.tensor_tensor(ss[:, s].rearrange("p (a b) m -> p a b m", a=2), sv[s],
                                        mx[:, s].unsqueeze(3).to_broadcast([P, 2, 2, L]),
                                        ALU.subtract).then_inc(Q["sub"], 1)

                def et_out(m):
                    wait(dve, Q["et_ps"], m.n() * 2 + 2)
                    wait(dve, Q["av_ps"], m.n())
                    v.tensor_copy(et[:, 1, :], b_3[:]).then_inc(Q["et_out1"], 1)

                def o_norm(m):
                    wait(dve, Q["av_ps"], m.n() + 1)
                    wait(dve, Q["oT"], m.n())
                    av = ps_o[:, :, 0:H * HS].rearrange("p s (h d) -> p s h d", h=H)
                    v.reciprocal(rinv[:], av[:, :, :, HD]).then_inc(Q["rinv"], 1)
                    wait(dve, Q["rinv"], m.n() + 1)
                    v.tensor_tensor(o[:], av[:, :, :, 0:HD], rinv[:].unsqueeze(3).to_broadcast([P, 2, H, HD]),
                                    ALU.mult).then_inc(Q["o"], 1)

                def y1(m):
                    p = m.slot(2)
                    wait(dve, Q["out_ps"], m.n() + 1)
                    wait(dve, Q["x2b"], m.n() + 1)
                    v.tensor_tensor(z[:], b_0[:].rearrange("p (s d) -> p s d", s=2), x2b[:, p], ALU.add).then_inc(Q["z"], 1)
                    wait(dve, Q["z"], m.n() + 1)
                    for s in range(2):
                        v.bn_stats(st_z[:, s, :], z[:, s, :]).then_inc(Q["zst"], 1)
                    wait(dve, Q["zst"], m.n() * 2 + 2)
                    apart(dve, passed["dve"])
                    for s in range(2):
                        v.bn_aggr(mv_z[:, s, :], st_z[:, s, :]).then_inc(Q["zmv"], 1)
                    wait(dve, Q["zmv"], m.n() * 2 + 2)
                    for s in range(2):
                        v.scalar_tensor_tensor(zg[:, s, :], z[:, s, :], mv_z[:, s, 0:1], r_g1, ALU.subtract,
                                               ALU.mult).then_inc(Q["zg"], 1)
                    wait(dve, Q["zrs"], m.n() + 1)
                    wait(dve, Q["zg"], m.n() * 2 + 2)
                    wait(dve, scattered[p], m.turn(2) * 32)
                    for s in range(2):
                        v.scalar_tensor_tensor(rows[:, p, s, 0:D], zg[:, s, :], rs_z[:, s:s + 1], r_be1, ALU.mult,
                                               ALU.add).then_inc(Q["y1"], 1)

                def route(m):
                    p = m.slot(2)
                    wait(dve, Q["logit_ps"], m.n() + 1)
                    v.tensor_reduce(lmax, logit, AX_X, ALU.max).then_inc(Q["lmax"], 1)
                    wait(dve, Q["lmax"], m.n() + 1)
                    v.tensor_tensor(dl[:], logit, lmax.unsqueeze(2).to_broadcast([P, 2, NE]),
                                    ALU.subtract).then_inc(Q["dlog"], 1)
                    wait(dve, Q["dlog"], m.n() + 1)
                    v.scalar_tensor_tensor(cand[:], dl[:], 0.0, rank8[:].unsqueeze(1).to_broadcast([P, 2, NE]),
                                           ALU.is_ge, ALU.mult).then_inc(Q["cand"], 1)
                    wait(dve, Q["cand"], m.n() + 1)
                    v.tensor_reduce(cmax, cand[:], AX_X, ALU.max).then_inc(Q["cmax"], 1)
                    wait(dve, Q["cmax"], m.n() + 1)
                    wait(dve, Q["order_ps"], m.n())
                    wait(dve, Q["ohcopy"], m.n())
                    v.tensor_tensor(oh[:], cand[:], cmax.unsqueeze(2).to_broadcast([P, 2, NE]),
                                    ALU.is_equal).then_inc(Q["onehot"], 1)
                    wait(dve, Q["elog"], m.n() + 1)
                    v.tensor_reduce(esum, el[:], AX_X, ALU.add).then_inc(Q["esum"], 1)
                    wait(dve, Q["esum"], m.n() + 1)
                    v.reciprocal(rows[:, p, :, OFF_GATE], esum).then_inc(Q["gate"], 1)

                def place(m):
                    wait(dve, Q["order_ps"], m.n() + 1)
                    for s in range(2):
                        v.tensor_tensor(oh_acc[:], oh_acc[:], oh[:, s, :], ALU.add).then_inc(Q["acc"], 1)
                        wait(dve, Q["acc"], m.n() * 2 + 1 + s)
                    v.tensor_tensor(pos[:], order, ebase[:].unsqueeze(1).to_broadcast([P, 2, NE]),
                                    ALU.add).then_inc(Q["pos"], 1)
                    wait(dve, Q["pos"], m.n() + 1)
                    v.tensor_tensor(pos[:], pos[:], oh[:], ALU.mult).then_inc(Q["posm"], 1)
                    wait(dve, Q["posm"], m.n() + 1)
                    wait(dve, Q["slot_i"], m.n())
                    v.tensor_reduce(slot_f, pos[:], AX_X, ALU.add).then_inc(Q["slot"], 1)

                def step(k):
                    for m, stage in ((k.back(2), o_lo), (k.back(-1), x_norm), (k.back(3), route), (k.back(2), y1),
                                     (k.back(1), et_out), (k.back(-1), x_lo), (k.back(3), place), (k, softmax),
                                     (k.back(1), o_norm)):
                        if m.valid(NG):
                            stage(m)

                run(dve, step, -1, NG + 3, 6, 48)

            @blk.tensor
            def _(pe):
                mm = nc.tensor.matmul

                def turn(dst, src, at):
                    for s in range(2):
                        for t in range(FT):
                            last = nc.tensor.transpose(dst[:, t * G + s * P:t * G + (s + 1) * P], src(s, t), ident[:])
                    return last

                def values(m):
                    wait(pe, Q["x2lo"], m.n() + 1)
                    wait(pe, Q["et_out1"], m.n() - 1)
                    for s in range(2):
                        last = product(b_3[:, s * D:(s + 1) * D],
                                       [(both(xh, xl, slice(None), slice(t * G + s * P, t * G + (s + 1) * P)),
                                         both(wh, wl, slice(None), slice(W_QKV + t * 3 * D + 2 * D, W_QKV + (t + 1) * 3 * D)))
                                        for t in range(FT)])
                    last.then_inc(Q["v_ps"], 1)

                def heads(m, dst, at, done):
                    for c in range(FT):
                        last = product(dst[:, c * G:(c + 1) * G],
                                       [(both(wh, wl, slice(None), slice(W_QKV + t * 3 * D + at + c * P,
                                                                         W_QKV + t * 3 * D + at + (c + 1) * P)),
                                         both(xh, xl, slice(None), slice(t * G, (t + 1) * G))) for t in range(FT)])
                    last.then_inc(Q[done], 1)

                def queries(m):
                    wait(pe, Q["o_lo"], m.n() - 1)
                    heads(m, b_1, 0, "q_ps")

                def keys(m):
                    wait(pe, Q["o"], m.n() - 1)
                    heads(m, b_2, D, "k_ps")

                def gate(m):
                    wait(pe, Q["y1T"], m.n() + 1)
                    wait(pe, Q["pos"], m.n())
                    for s in range(2):
                        for t in range(FT):
                            last = mm(logit[:, s, :], y1t[:, t * G + s * P:t * G + (s + 1) * P], wg_sb[:, t, :],
                                      start=(t == 0), stop=(t == FT - 1))
                    last.then_inc(Q["logit_ps"], 1)

                def project(m):
                    wait(pe, Q["o_lo"], m.n() + 1)
                    wait(pe, Q["y1T"], m.n())
                    for s in range(2):
                        last = product(b_0[:, s * D:(s + 1) * D],
                                       [(both(oh_, ol_, slice(None), slice(t * G + s * P, t * G + (s + 1) * P)),
                                         both(wh, wl, slice(None), slice(W_OUT + t * D, W_OUT + (t + 1) * D)))
                                        for t in range(FT)])
                    last.then_inc(Q["out_ps"], 1)

                def turn_e(m):
                    wait(pe, Q["exp"], m.n() * 2 + 2)
                    wait(pe, Q["q_out"], m.n() * 2 + 4, 2 * NG)
                    for s, dst in ((0, b_1), (1, b_3)):
                        if s == 1:
                            wait(pe, Q["v_out"], m.n() + 2, NG)
                        for c in range(H):
                            last = nc.tensor.transpose(dst[:, c * P:(c + 1) * P], eb[:, s, c, :], ident[:])
                        last.then_inc(Q["et_ps"], 1)

                def turn_x(m):
                    wait(pe, Q["x2"], m.n() * 2 + 2)
                    wait(pe, Q["k_out"], m.n() * 2)
                    p = m.slot(2)
                    turn(b_2, lambda s, t: x2[:, p, s, t * P:(t + 1) * P], 0).then_inc(Q["x2T"], 1)

                def scores(m):
                    wait(pe, Q["q_out"], m.n() * 2 + 2)
                    wait(pe, Q["k_out"], m.n() * 2 + 2)
                    wait(pe, Q["sub"], m.n() * 2)
                    apart(pe, passed["pe"])
                    for s in range(2):
                        for t in range(2):
                            for hh in range(H):
                                b, a = hh // 2, hh % 2
                                r, c = slice(a * HD, (a + 1) * HD), slice(b * G + s * P + t * L, b * G + s * P + (t + 1) * L)
                                last = mm(ps_s[t * L:(t + 1) * L, a, s * 2 * L + b * L:s * 2 * L + (b + 1) * L],
                                          q[r, c], kk[r, c], start=True, stop=True)
                    last.then_inc(Q["s_ps"], 1)

                def rank(m):
                    wait(pe, Q["onehot"], m.n() + 1)
                    wait(pe, Q["dlog"], m.n() + 1)
                    wait(pe, Q["acc"], m.n() * 2)
                    mm(order[:, 0, :], before[:], oh[:, 0, :], start=True, stop=False)
                    mm(order[:, 0, :], ones_b[:], oh_acc[:], start=False, stop=True)
                    mm(order[:, 1, :], before[:], oh[:, 1, :], start=True, stop=False)
                    mm(order[:, 1, :], ones_b[:], oh[:, 0, :], start=False, stop=False)
                    mm(order[:, 1, :], ones_b[:], oh_acc[:], start=False, stop=True).then_inc(Q["order_ps"], 1)

                def attend(m):
                    wait(pe, Q["et_out0"], m.n() + 1)
                    wait(pe, Q["et_out1"], m.n() + 1)
                    wait(pe, Q["o"], m.n())
                    wait(pe, Q["x2lo"], m.n() + 3, NG)
                    p = m.slot(2)
                    for s in range(2):
                        for hh in range(H):
                            c = (hh % 2) * 2 + hh // 2
                            last = mm(ps_o[:, s, hh * HS:(hh + 1) * HS], et[:, s, c * P:(c + 1) * P], va[:, p, s, hh, :],
                                      start=True, stop=True)
                    last.then_inc(Q["av_ps"], 1)

                def turn_y(m):
                    wait(pe, Q["y1"], m.n() * 2 + 2)
                    p = m.slot(2)
                    turn(b_0, lambda s, t: rows[:, p, s, t * P:(t + 1) * P], 0).then_inc(Q["y1T_ps"], 1)

                def turn_o(m):
                    wait(pe, Q["o"], m.n() + 1)
                    of = o[:].rearrange("p s h d -> p s (h d)")
                    turn(b_1, lambda s, t: of[:, s, t * P:(t + 1) * P], 0).then_inc(Q["oT"], 1)

                def step(k):
                    for m, stage in ((k, values), (k.back(3), gate), (k, queries), (k, keys), (k.back(2), project),
                                     (k.back(1), turn_e), (k.back(-1), turn_x), (k, scores), (k.back(3), rank),
                                     (k.back(1), attend), (k.back(2), turn_y), (k.back(1), turn_o)):
                        if m.valid(NG):
                            stage(m)

                run(pe, step, -1, NG + 3, 6, 48)

        with ExitStack() as pc:
            def pb(name, shape):
                return pc.enter_context(nc.psum_tensor(name, shape, F32))

            J = 2 * NG
            oht = sb("oht", [P, NE, J], F32, pc)
            cinc = sb("cinc", [P, NE, J], F32, pc)
            cexc = sb("cexc", [P, NE, J], F32, pc)
            tot = sb("tot", [P, NE, J], F32, pc)
            ones_j = sb("ones_j", [P, J], F32, pc)
            s1 = sb("s1", [P, J], F32, pc)
            kmax = sb("kmax", [P, NE], F32, pc)
            thr = sb("thr", [P, NE], F32, pc)
            cnt = sb("cnt", [P, NE], F32, pc)
            ci = sb("ci", [P, NE], I32, pc)
            fi = sb("fi", [P, NE], I32, pc)
            nt = sb("nt", [P, 4, NE], F32, pc)
            nti = sb("nti", [P, NE], I32, pc)
            one8 = sb("one8", [P, NE], F32, pc)
            tix_i, tix = sb("tix_i", [P, TILES], I32, pc), sb("tix", [P, TILES], F32, pc)
            ge, gw = sb("ge", [P, TILES, NE], F32, pc), sb("gw", [P, TILES, NE], F32, pc)
            tile_e, tile_r = sb("tile_e", [P, TILES], F32, pc), sb("tile_r", [P, TILES], F32, pc)
            tab_e, tab_r = sb("tab_e", [P, TILES], I32, pc), sb("tab_r", [P, TILES], I32, pc)
            row = sb("row", [P, 4, ROW], F32, pc)
            yt = sb("yt", [P, 2, FT * P], F32, pc)
            hb = sb("c_hb", [P, 4, D], F32, pc)
            sidx = sb("sidx", [P, 4], I32, pc)
            gk = sb("gk", [P, 2], F32, pc)
            tb, z = sb("tb", [P, 2, D], F32, pc), sb("c_z", [P, 2, D], F32, pc)
            st, mv = sb("c_st", [P, 2, 6], F32, pc), sb("c_mv", [P, 2, 2], F32, pc)
            ve, rs = sb("c_ve", [P, 2], F32, pc), sb("c_rs", [P, 2], F32, pc)
            zg = sb("c_zg", [P, D], F32, pc)
            res = sb("res", [P, 4, D], F32, pc)
            ps_l = [pb(f"ps_l{i}", [P, 4, J]) for i in range(2)]
            ps_c = pb("ps_c", [P, NE])
            ps_t = [pb(f"c_ps_t{i}", [P, FT * P]) for i in range(2)]
            ps_y = [pb(f"c_ps_y{i}", [P, D]) for i in range(2)]

            own, cnt_ps, cexc_ready, loc_ps = (sem("c_" + s) for s in ("own", "count_ps", "ranks_in", "rank_ps"))
            kmax_ready, thr_ready, tab_ready, filled, tiota, fi_ready = (
                sem("c_" + s) for s in ("kmax", "threshold", "tables", "filled", "tile_iota", "fill_rows"))
            loaded = [sem(f"c_loaded{i}") for i in range(4)]
            sent = [sem(f"c_sent{i}") for i in range(4)]
            (yt_ps, yt_out, mm_ps, gk_s, tb_s, z_s, st_s, mv_s, ve_s, rs_s, zg_s, res_s, hb_s, idx_s) = (
                sem("c_" + s) for s in ("yT_ps", "yT", "expert_ps", "gk", "tb", "z", "st", "mv", "ve", "rs", "zg",
                                        "res", "hb", "idx"))
            blk = pc.enter_context(nc.Block())

            @blk.sync
            def _(sp):
                sp.dma_start(bins[BINS:BINS + P, :], fill[:]).then_inc(filled, 16)
                sp.wait_ge(fi_ready, 1)
                for e in range(NE):
                    r = sp.value_load(fi[0:1, e:e + 1], min_val=0, max_val=BINS)
                    sp.dma_start(bins[bass.ds(r, P), :], fill[:]).then_inc(filled, 16)
                sp.wait_ge(filled, 16 * (NE + 1))
                sp.wait_ge(tab_ready, 1)

                def load(k):
                    wait(sp, sent[k.slot(4)], k.turn(4) * 16)
                    r = sp.value_load(tab_r[0:1, bass.ds(k.n(), 1)], min_val=0, max_val=BINS)
                    sp.dma_start(row[:, k.slot(4), :], bins[bass.ds(r, P), :]).then_inc(loaded[k.slot(4)], 16)

                run(sp, load, 0, TILES, 8, TILES - 4, 4)

            @blk.scalar
            def _(act):
                def y_out(k):
                    wait(act, yt_ps, k.n() + 1)
                    wait(act, mm_ps, k.n() - 1)
                    nc.scalar.activation(yt[:, k.slot(2), :], ps_t[k.slot(2)][:], ACT.Copy).then_inc(yt_out, 1)

                run(act, y_out, 0, TILES, 8, TILES - 4, 4)

            @blk.gpsimd
            def _(pool):
                g = nc.gpsimd
                g.iota(tix_i[:], [[1, TILES]], base=0, channel_multiplier=0).then_inc(tiota, 1)
                pool.wait_ge(kmax_ready, 1)
                g.partition_all_reduce(thr[:], kmax[:], P, bass.bass_isa.ReduceOp.max).then_inc(thr_ready, 1)

                def prepare(k):
                    b, p = k.slot(4), k.slot(2)
                    wait(pool, loaded[b], (k.turn(4) + 1) * 16)
                    wait(pool, sent[b], k.turn(4) * 16)
                    apart(pool, passed["pool"])
                    g.tensor_copy(sidx[:, b:b + 1], row[:, b, OFF_S:OFF_S + 1]).then_inc(idx_s, 1)
                    wait(pool, res_s, k.n() - 3)
                    g.tensor_tensor(hb[:, b, :], row[:, b, D:2 * D], r_be2, ALU.add).then_inc(hb_s, 1)

                def rstd(k):
                    p = k.slot(2)
                    wait(pool, mv_s, k.n() + 1)
                    wait(pool, res_s, k.n() - 1)
                    apart(pool, passed["pool"])
                    g.tensor_scalar(ve[:, p:p + 1], mv[:, p, 1:2], EPS, None, ALU.add).then_inc(ve_s, 1)
                    wait(pool, ve_s, k.n() + 1)
                    g.tensor_tensor(rs[:, p:p + 1], ve[:, p:p + 1], mhalf[:, 0:1], ALU.pow).then_inc(rs_s, 1)

                def send(k):
                    b = k.slot(4)
                    wait(pool, res_s, k.n() + 1)
                    wait(pool, idx_s, k.n() + 1)
                    apart(pool, passed["pool"])
                    g.indirect_dma_start(out, bass.IndirectOffsetOnAxis(ap=sidx[:, b:b + 1], axis=0), res[:, b, :],
                                         None, bounds_check=S - 1, oob_is_err=False).then_inc(sent[b], 16)

                def step(k):
                    for m, stage in ((k, prepare), (k.back(1), rstd), (k.back(3), send)):
                        if m.valid(TILES):
                            stage(m)

                run(pool, step, 0, TILES + 3, 8, TILES - 4, 4)
                for i in range(4):
                    pool.wait_ge(sent[i], 16 * (TILES // 4))

            @blk.vector
            def _(dve):
                v = nc.vector
                count = [0]

                def link(ins):
                    count[0] += 1
                    ins.then_inc(own, 1)
                    dve.wait_ge(own, count[0])

                dve.wait_ge(cnt_ps, 1)
                link(v.tensor_copy(cnt[:], ps_c[:]))
                link(v.tensor_tensor(nt[:, 0, :], cnt[:], ebase[:], ALU.add))
                v.tensor_copy(fi[:], nt[:, 0, :]).then_inc(fi_ready, 1)
                link(v.tensor_scalar(cnt[:], cnt[:], float(P - 1), None, ALU.add))
                link(v.tensor_copy(ci[:], cnt[:]))
                link(v.tensor_scalar(nti[:], ci[:], 7, None, ALU.arith_shift_right))
                link(v.tensor_copy(nt[:, 1, :], nti[:]))
                link(v.memset(one8[:], 1.0))
                link(v.tensor_tensor_scan(nt[:, 2, :], one8[:], nt[:, 1, :], 0.0, ALU.mult, ALU.add))
                link(v.tensor_scalar(nt[:, 3, :], nt[:, 1, :], -float(P), float(BIN), ALU.mult, ALU.add))
                dve.wait_ge(tiota, 1)
                link(v.tensor_copy(tix[:], tix_i[:]))
                link(v.tensor_tensor(ge[:], tix[:].unsqueeze(2).to_broadcast([P, TILES, NE]),
                                     nt[:, 2, :].unsqueeze(1).to_broadcast([P, TILES, NE]), ALU.is_ge))
                link(v.tensor_tensor(gw[:], ge[:], nt[:, 3, :].unsqueeze(1).to_broadcast([P, TILES, NE]), ALU.mult))
                link(v.tensor_reduce(tile_e[:], ge[:], AX_X, ALU.add))
                link(v.tensor_reduce(tile_r[:], gw[:], AX_X, ALU.add))
                link(v.tensor_scalar(tix[:], tix[:], float(P), None, ALU.mult))
                link(v.tensor_tensor(tile_r[:], tile_r[:], tix[:], ALU.add))
                link(v.tensor_scalar(tab_r[:], tile_r[:], float(BINS), None, ALU.min))
                v.tensor_scalar(tab_e[:], tile_e[:], float(NE - 1), None, ALU.min).then_inc(tab_ready, 1)
                link(v.memset(ones_j[:], 1.0))
                link(v.tensor_copy(oht[:], oh_all[:].rearrange("p j e -> p e j")))
                for e in range(NE):
                    last = v.tensor_tensor_scan(cinc[:, e, :], ones_j[:], oht[:, e, :], 0.0, ALU.mult, ALU.add)
                link(last)
                link(v.tensor_tensor(cexc[:], cinc[:], oht[:], ALU.subtract))
                v.tensor_copy(tot[:], cinc[:, :, J - 1:J].to_broadcast([P, NE, J])).then_inc(cexc_ready, 1)
                link(v.tensor_scalar(s1[:], s_tab[:], 1.0, None, ALU.add))
                dve.wait_ge(loc_ps, 1)
                for i in range(2):
                    link(v.scalar_tensor_tensor(cexc[:, 4 * i:4 * i + 4, :], ps_l[i][:], float(CAP),
                                                oht[:, 4 * i:4 * i + 4, :], ALU.is_lt, ALU.mult))
                link(v.tensor_tensor(cexc[:], cexc[:], s1[:].unsqueeze(1).to_broadcast([P, NE, J]), ALU.mult))
                v.tensor_reduce(kmax[:], cexc[:], AX_X, ALU.max).then_inc(kmax_ready, 1)
                dve.wait_ge(thr_ready, 1)
                dve.wait_ge(tab_ready, 1)

                def expert(k):
                    b, p = k.slot(4), k.slot(2)
                    e = dve.value_load(tab_e[0:1, bass.ds(k.n(), 1)], min_val=0, max_val=NE - 1)
                    wait(dve, loaded[b], (k.turn(4) + 1) * 16)
                    v.tensor_scalar(gk[:, p:p + 1], row[:, b, OFF_S:OFF_S + 1], thr[:, bass.ds(e, 1)],
                                    row[:, b, OFF_GATE:OFF_GATE + 1], ALU.is_lt, ALU.mult).then_inc(gk_s, 1)
                    wait(dve, mm_ps, k.n() + 1)
                    v.tensor_tensor(tb[:, p, :], ps_y[p][:], b12[:, bass.ds(e, 1), :].rearrange("p a d -> p (a d)"),
                                    ALU.add).then_inc(tb_s, 1)
                    wait(dve, tb_s, k.n() + 1)
                    wait(dve, gk_s, k.n() + 1)
                    v.scalar_tensor_tensor(z[:, p, :], tb[:, p, :], gk[:, p:p + 1], row[:, b, 0:D], ALU.mult,
                                           ALU.add).then_inc(z_s, 1)
                    wait(dve, z_s, k.n() + 1)
                    v.bn_stats(st[:, p, :], z[:, p, :]).then_inc(st_s, 1)
                    wait(dve, st_s, k.n() + 1)
                    apart(dve, passed["dve"])
                    v.bn_aggr(mv[:, p, :], st[:, p, :]).then_inc(mv_s, 1)

                def finish(k):
                    b, p = k.slot(4), k.slot(2)
                    wait(dve, mv_s, k.n() + 1)
                    wait(dve, res_s, k.n())
                    v.scalar_tensor_tensor(zg[:], z[:, p, :], mv[:, p, 0:1], r_g2, ALU.subtract,
                                           ALU.mult).then_inc(zg_s, 1)
                    wait(dve, zg_s, k.n() + 1)
                    wait(dve, rs_s, k.n() + 1)
                    wait(dve, hb_s, k.n() + 1)
                    wait(dve, sent[b], k.turn(4) * 16)
                    v.scalar_tensor_tensor(res[:, b, :], zg[:], rs[:, p:p + 1], hb[:, b, :], ALU.mult,
                                           ALU.add).then_inc(res_s, 1)

                def step(k):
                    for m, stage in ((k, expert), (k.back(1), finish)):
                        if m.valid(TILES):
                            stage(m)

                run(dve, step, 0, TILES + 1, 8, TILES - 4, 4)

            @blk.tensor
            def _(pe):
                mm = nc.tensor.matmul
                mm(ps_c[:], ones_b[:], oh_acc[:], start=True, stop=True).then_inc(cnt_ps, 1)
                pe.wait_ge(cexc_ready, 1)
                for i in range(2):
                    for c in range(4):
                        e = 4 * i + c
                        mm(ps_l[i][:, c, :], later_l[:], tot[:, e, :], start=True, stop=False)
                        mm(ps_l[i][:, c, :], same_l[:], cexc[:, e, :], start=False, stop=False)
                        last = mm(ps_l[i][:, c, :], first_n[:], oht[:, e, :], start=False, stop=True)
                last.then_inc(loc_ps, 1)
                pe.wait_ge(tab_ready, 1)

                def turn_y(k):
                    b = k.slot(4)
                    wait(pe, loaded[b], (k.turn(4) + 1) * 16)
                    wait(pe, yt_out, k.n() - 1)
                    for t in range(FT):
                        last = nc.tensor.transpose(ps_t[k.slot(2)][:, t * P:(t + 1) * P], row[:, b, t * P:(t + 1) * P],
                                                   ident[:])
                    last.then_inc(yt_ps, 1)

                def expert(k):
                    e = pe.value_load(tab_e[0:1, bass.ds(k.n(), 1)], min_val=0, max_val=NE - 1)
                    p = k.slot(2)
                    wait(pe, yt_out, k.n() + 1)
                    wait(pe, tb_s, k.n() - 1)
                    for t in range(FT):
                        last = mm(ps_y[p][:], yt[:, p, t * P:(t + 1) * P],
                                  w12[:, bass.ds(e, 1), t * D:(t + 1) * D].rearrange("p a d -> p (a d)"),
                                  start=(t == 0), stop=(t == FT - 1))
                    last.then_inc(mm_ps, 1)

                def step(k):
                    for m, stage in ((k, turn_y), (k.back(1), expert)):
                        if m.valid(TILES):
                            stage(m)

                run(pe, step, 0, TILES + 1, 8, TILES - 4, 4)


def kernel(**inputs):
    import numpy as np
    import concourse.bacc as bacc
    from concourse.bass_utils import run_bass_kernel_spmd

    a = {k: np.asarray(v) for k, v in inputs.items()}

    def blocks(w, width):
        t = w.T.reshape(-1, 128, width)
        return np.ascontiguousarray(t.transpose(1, 0, 2).reshape(128, -1))

    def cols(v):
        return np.ascontiguousarray(v.reshape(-1, 128).T)

    x = a["x"].reshape(L, 3, 14, 16, 14, 16).transpose(0, 1, 2, 4, 3, 5).reshape(NG, G, KT, P)
    arrays = {
        "xt": np.ascontiguousarray(x.transpose(0, 3, 2, 1).reshape(NG, P, KT * G)),
        "w_tok": blocks(a["L0_tok_W"], D), "b_tok": a["L0_tok_b"],
        "log_a": cols(a["L0_attn_log_A"]), "w_b": blocks(a["L0_attn_W_B"], D), "b_b": cols(a["L0_attn_b_B"]),
        "w_c": blocks(a["L0_attn_W_C"], D), "b_c": a["L0_attn_b_C"],
        "w_d": blocks(a["L0_attn_W_D"], D), "b_d": a["L0_attn_b_D"], "log_dt": a["L0_attn_log_dt"],
        "w_in": blocks(a["L0_ffn_in_proj_w"], 3 * D), "b_qk": cols(a["L0_ffn_in_proj_b"][:2 * D]),
        "b_v": cols(a["L0_ffn_in_proj_b"][2 * D:]),
        "w_o": blocks(a["L0_ffn_out_proj_w"], D), "b_o": a["L0_ffn_out_proj_b"],
        "g1": a["L0_ffn_ln1_g"], "be1": a["L0_ffn_ln1_b"], "g2": a["L0_ffn_ln2_g"], "be2": a["L0_ffn_ln2_b"],
        "wg": np.ascontiguousarray(a["L0_ffn_wg"].reshape(FT, P, NE).transpose(1, 0, 2).reshape(P, FT * NE)),
        "w1t": np.ascontiguousarray(a["L0_ffn_w1"].transpose(0, 2, 1).reshape(NE, FK, P, D)
                                    .transpose(0, 2, 1, 3).reshape(NE, P, FK * D)),
        "b1c": cols(a["L0_ffn_b1"]),
        "w2": np.ascontiguousarray(a["L0_ffn_w2"].reshape(NE, FK, P, D).transpose(0, 2, 1, 3).reshape(NE, P, FK * D)),
        "b2c": cols(a["L0_ffn_b2"]),
    }
    nc = bacc.Bacc("TRN2", target_bir_lowering=False, num_devices=1)
    given = {}
    for name, v in arrays.items():
        arrays[name] = np.ascontiguousarray(v)
        given[name] = nc.dram_tensor(name, v.shape, mybir.dt.from_np(v.dtype), kind="ExternalInput").ap()
    out = nc.dram_tensor("out", (S, D), F32, kind="ExternalOutput").ap()
    build(nc, out=out, **given)
    r = run_bass_kernel_spmd(nc, [arrays], core_ids=[0])
    return r.results[0]["out"].reshape(L, N, D)
```

```python
import concourse.bass as bass
from concourse import mybir
from contextlib import ExitStack

F32 = mybir.dt.float32
F32R = mybir.dt.float32r
BF16 = mybir.dt.bfloat16
I32 = mybir.dt.int32
ALU = mybir.AluOpType
ACT = mybir.ActivationFunctionType
AX_X = mybir.AxisListType.X

P = 128
L, N = 64, 196
S = L * N
D = 256
FT = D // P
KP = 768
KT = KP // P
H, HD = 4, 64
HS = HD + 1
NE, FF = 8, 1024
FK = FF // P
CAP = S // NE
EPS = 1e-5
G = 2 * P
NG = S // G
BIN = S + P
BINS = NE * BIN
TILES = 6 * -(-(S // P + NE) // 6)
FOLD = 6
ROW = 2 * D + 2
OFF_GATE, OFF_S = 2 * D, 2 * D + 1
FAR = float(2 * S)

W_TOK = 0
W_B = W_TOK + KT * D
W_C = W_B + FT * D
W_D = W_C + FT * D
W_QKV = W_D + FT * D
W_OUT = W_QKV + FT * 3 * D
WCOLS = W_OUT + FT * D


class At:

    def __init__(self, t, c, u=2):
        self.t, self.c, self.u = t, c, u

    def back(self, s):
        return At(self.t, self.c - s, self.u)

    def n(self):
        return self.c if isinstance(self.t, int) else self.t * self.u + self.c

    def slot(self, r):
        return self.c % r

    def turn(self, r):
        return self.c // r if isinstance(self.t, int) else self.t * (self.u // r) + self.c // r

    def valid(self, count):
        return not isinstance(self.t, int) or 0 <= self.c < count


def wait(eng, sem, value, most=None):
    if isinstance(value, int):
        if most is not None:
            value = min(value, most)
        if value <= 0:
            return
    eng.wait_ge(sem, value)


def apart(eng, passed):
    eng.sem_inc(passed, 1)


def run(eng, step, first, last, lo, hi, u=2):
    for c in range(first, lo):
        step(At(0, c, u))
    with eng.Fori(0, (hi - lo) // u) as t:
        for c in range(u):
            step(At(t, lo + c, u))
    for c in range(hi, last):
        step(At(0, c, u))


def build(nc, xt, w_tok, b_tok, log_a, w_b, b_b, w_c, b_c, w_d, b_d, log_dt, w_in, b_qk, b_v, w_o, b_o,
          g1, be1, g2, be2, wg, w1t, w2, b2c, out):
    h1_dram = nc.dram_tensor("h1_dram", (S, D), F32, kind="Internal").ap()
    x2_dram = nc.dram_tensor("x2_dram", (S, D), F32, kind="Internal").ap()
    bins = nc.dram_tensor("bins", (BINS + P, ROW), F32, kind="Internal").ap()
    with ExitStack() as ctx:
        def sb(name, shape, dt=F32, c=ctx):
            return c.enter_context(nc.sbuf_tensor(name, shape, dt))

        def sem(name):
            return ctx.enter_context(nc.semaphore(name))

        wh, wl = sb("wh", [P, WCOLS], F32R), sb("wl", [P, WCOLS], F32R)
        w12 = sb("w12", [P, NE, FT * D])
        b12 = sb("b12", [1, NE, D])
        one_row = sb("one_row", [1, P])
        rows_c = sb("rows_c", [P, 8, D])
        r_btok, r_bcd, r_bo, r_g1, r_be1, r_g2, r_be2, r_bd = (rows_c[:, i, :] for i in range(8))
        cols_c = sb("cols_c", [P, 16])
        c_loga, c_bb, c_bqk, c_bv, c_dt = (cols_c[:, a:b] for a, b in ((0, 2), (2, 4), (4, 8), (8, 10), (10, 11)))
        c_a, c_bbdt = cols_c[:, 11:13], cols_c[:, 13:15]
        ident = sb("ident", [P, P])
        decay = sb("decay", [P, FT, G + N])
        wg_sb = sb("wg_sb", [P, FT, NE])
        mhalf = sb("mhalf", [P, 2])
        c_eps = sb("c_eps", [P, 1])
        before = sb("before", [P, P], BF16)
        ones_b = sb("ones_b", [P, P], BF16)
        later_l = sb("later_l", [P, P])
        same_l = sb("same_l", [P, P])
        first_n = sb("first_n", [P, P])
        ebase = sb("ebase", [P, NE])
        rank8 = sb("rank8", [P, NE])
        s_tab = sb("s_tab", [P, 2 * NG])
        oh_all = sb("oh_all", [P, 2 * NG, NE], BF16)
        oh_acc = sb("oh_acc", [P, NE], BF16)
        fill = sb("fill", [P, ROW])

        with ExitStack() as pre:
            wf = sb("wf", [P, WCOLS], F32, pre)
            colf = sb("colf", [P, P], F32, pre)
            coli = sb("coli", [P, P], I32, pre)
            parti = sb("parti", [P, 2], I32, pre)
            partf = sb("partf", [P, 4], F32, pre)
            lcoli = sb("lcoli", [P, P], I32, pre)
            lcolf = sb("lcolf", [P, P], F32, pre)
            tmp8 = sb("tmp8", [P, NE], I32, pre)
            tmpe = sb("tmpe", [P, NE], I32, pre)
            stabi = sb("stabi", [P, 2 * NG], I32, pre)
            bvb = sb("bvb", [P, FT, P], F32, pre)
            ps_bo = pre.enter_context(nc.psum_tensor("ps_bo", [P, D], F32))
            passed = {e: sem("passed_" + e) for e in ("pool", "dve", "pe")}
            w_in_sem, c_in_sem = sem("w_loaded"), sem("consts_loaded")
            hi_done, pre_iota, own, act_own = sem("w_hi_done"), sem("iota_done"), sem("pre_dve"), sem("pre_act")
            bo_ready, bo_done, dt_col = sem("bv_spread"), sem("bo_product"), sem("dt_done")
            a_arg = sem("decay_arg")
            blk = pre.enter_context(nc.Block())

            @blk.sync
            def _(sp):
                for off, src in ((W_TOK, w_tok), (W_B, w_b), (W_C, w_c), (W_D, w_d), (W_QKV, w_in), (W_OUT, w_o)):
                    width = src.shape[1]
                    sp.dma_start(wf[:, off:off + width], src).then_inc(w_in_sem, 16)

            @blk.scalar
            def _(act):
                n = 0
                for dst, src in ((c_loga, log_a), (c_bb, b_b), (c_bqk, b_qk), (c_bv, b_v),
                                 (wg_sb[:].rearrange("p t e -> p (t e)"), wg)):
                    act.dma_start(dst, src).then_inc(c_in_sem, 16)
                for dst, src in ((r_btok, b_tok), (r_bcd, b_c), (r_bd, b_d), (r_bo, b_o), (r_g1, g1), (r_be1, be1),
                                 (r_g2, g2), (r_be2, be2), (c_dt, log_dt)):
                    act.dma_start(dst, src.partition_broadcast(P)).then_inc(c_in_sem, 16)
                act.wait_ge(c_in_sem, 14 * 16)
                nc.scalar.activation(c_dt, c_dt, ACT.Exp).then_inc(dt_col, 1)
                nc.scalar.activation(c_a, c_loga, ACT.Exp).then_inc(dt_col, 1)
                act.wait_ge(a_arg, 1)
                nc.scalar.activation(c_a, c_a, ACT.Exp).then_inc(act_own, 1)
                act.wait_ge(w_in_sem, 6 * 16)
                nc.scalar.activation(wh[:], wf[:], ACT.Copy).then_inc(hi_done, 1)

            @blk.gpsimd
            def _(pool):
                nc.gpsimd.iota(coli[:], [[1, P]], base=0, channel_multiplier=0).then_inc(pre_iota, 1)
                nc.gpsimd.iota(lcoli[:], [[0, 2], [1, L]], base=0, channel_multiplier=0).then_inc(pre_iota, 1)
                nc.gpsimd.iota(parti[:, 0:1], [[1, 1]], base=0, channel_multiplier=1).then_inc(pre_iota, 1)
                nc.gpsimd.iota(tmp8[:], [[-1, NE]], base=NE, channel_multiplier=0).then_inc(pre_iota, 1)
                nc.gpsimd.iota(tmpe[:], [[BIN, NE]], base=0, channel_multiplier=0).then_inc(pre_iota, 1)
                nc.gpsimd.iota(stabi[:], [[2, 2 * NG]], base=0, channel_multiplier=N).then_inc(pre_iota, 1)

            @blk.tensor
            def _(pe):
                pe.wait_ge(bo_ready, 1)
                pe.wait_ge(w_in_sem, 6 * 16)
                for t in range(FT):
                    last = nc.tensor.matmul(ps_bo[:], bvb[:, t, :], wf[:, W_OUT + t * D:W_OUT + (t + 1) * D],
                                            start=(t == 0), stop=(t == FT - 1))
                last.then_inc(bo_done, 1)

            @blk.vector
            def _(dve):
                v = nc.vector
                count = [0]

                def link(ins):
                    count[0] += 1
                    ins.then_inc(own, 1)
                    dve.wait_ge(own, count[0])

                v.memset(mhalf[:], -0.5)
                v.memset(c_eps[:], EPS)
                v.memset(one_row[:], 1.0)
                v.memset(ones_b[:], 1.0)
                v.memset(oh_acc[:], 0.0)
                v.memset(fill[:, 0:OFF_S], 0.0)
                v.memset(fill[:, OFF_S:ROW], FAR)
                dve.wait_ge(pre_iota, 6)
                link(v.tensor_copy(colf[:], coli[:]))
                link(v.tensor_copy(lcolf[:], lcoli[:]))
                link(v.tensor_copy(partf[:, 0:1], parti[:, 0:1]))
                v.tensor_copy(rank8[:], tmp8[:])
                v.tensor_copy(ebase[:], tmpe[:])
                link(v.tensor_copy(s_tab[:], stabi[:]))
                link(v.tensor_scalar(partf[:, 1:2], partf[:, 0:1], float(L), None, ALU.is_ge))
                link(v.scalar_tensor_tensor(partf[:, 2:3], partf[:, 1:2], -float(L), partf[:, 0:1], ALU.mult, ALU.add))
                v.tensor_scalar(ident[:], colf[:], partf[:, 0:1], None, ALU.is_equal)
                v.tensor_scalar(before[:], colf[:], partf[:, 0:1], None, ALU.is_gt)
                v.tensor_scalar(later_l[:], lcolf[:], partf[:, 2:3], None, ALU.is_gt)
                link(v.tensor_scalar(same_l[:], lcolf[:], partf[:, 2:3], None, ALU.is_equal))
                link(v.tensor_scalar(partf[:, 3:4], partf[:, 1:2], 1.0 - float(L * N), None, ALU.mult))
                link(v.tensor_scalar(s_tab[:], s_tab[:], partf[:, 3:4], None, ALU.add))
                link(v.tensor_scalar(partf[:, 3:4], partf[:, 1:2], -1.0, 1.0, ALU.mult, ALU.add))
                link(v.tensor_scalar(colf[:], colf[:], float(L), None, ALU.is_ge))
                link(v.tensor_scalar(first_n[:], colf[:], partf[:, 3:4], None, ALU.mult))
                link(v.tensor_tensor(first_n[:], first_n[:], same_l[:], ALU.mult))
                dve.wait_ge(c_in_sem, 14 * 16)
                link(v.tensor_tensor(r_bcd, r_bcd, r_bd, ALU.add))
                link(v.tensor_copy(bvb[:], c_bv.unsqueeze(2).to_broadcast([P, FT, P])))
                v.engine_nop().then_inc(bo_ready, 1)
                dve.wait_ge(dt_col, 2)
                v.tensor_scalar(c_bbdt, c_bb, c_dt, None, ALU.mult)
                v.tensor_scalar(c_a, c_a, c_dt, -1.0, ALU.mult, ALU.mult).then_inc(a_arg, 1)
                dve.wait_ge(act_own, 1)
                link(v.tensor_copy(decay[:], c_a.unsqueeze(2).to_broadcast([P, FT, G + N])))
                link(v.memset(decay[:, :, 0:G + N:N], 0.0))
                dve.wait_ge(bo_done, 1)
                link(v.tensor_tensor(r_bo, r_bo, ps_bo[:], ALU.add))
                dve.wait_ge(hi_done, 1)
                link(v.tensor_tensor(wl[:], wf[:], wh[:].bitcast(F32), ALU.subtract))

        def product(out_ps, pairs):
            terms = [(a, b) for (ah, al), (bh, bl) in pairs for a, b in ((ah, bh), (ah, bl), (al, bh))]
            for i, (a, b) in enumerate(terms):
                last = nc.tensor.matmul(out_ps, a, b, start=(i == 0), stop=(i == len(terms) - 1))
            return last

        def both(a, b, *idx):
            return a[idx], b[idx]

        with ExitStack() as pa:
            def pb(name, shape):
                return pa.enter_context(nc.psum_tensor(name, shape, F32))

            xf = sb("xf", [P, 2, KT * G], F32, pa)
            xh, xl = sb("xh", [P, 2, KT * G], F32R, pa), sb("xl", [P, 2, KT * G], F32R, pa)
            h = sb("h", [P, 2, 2, D], F32, pa)
            hb = sb("hb", [P, 3, 2, D], F32, pa)
            u = sb("u", [P, 2, 2, D], F32, pa)
            uh, ul = sb("uh", [P, 2, FT * G], F32R, pa), sb("ul", [P, 2, FT * G], F32R, pa)
            bu = sb("bu", [P, 2, FT, G], F32, pa)
            xs = sb("xs", [P, 2, FT, G], F32, pa)
            sh, sl = sb("sh", [P, 2, FT * G], F32R, pa), sb("sl", [P, 2, FT * G], F32R, pa)
            h1o = sb("h1o", [P, 2, 2, D], F32, pa)
            x2o = sb("x2o", [P, 2, 2, D], F32, pa)
            stats, st_x = sb("stats_a", [P, 2, 6], F32, pa), sb("stats_x", [P, 2, 6], F32, pa)
            mv, mv_x = sb("mv_a", [P, 2, 2], F32, pa), sb("mv_xa", [P, 2, 2], F32, pa)
            nrm, nrm_x = sb("nrm_a", [P, 3, 2], F32, pa), sb("nrm_x", [P, 3, 2], F32, pa)
            h1b = sb("h1b", [P, 2, 2, D], F32, pa)
            w1s = sb("w1s", [P, FK * D], F32, pa)
            w2s = sb("w2s", [P, FK * D + FK], F32, pa)
            ps_h = [pb(f"ps_h{i}", [P, D]) for i in range(2)]
            ps_t = pb("ps_t", [P, FT * G])
            ps_b = pb("ps_b", [P, FT * G])
            ps_y = [pb(f"ps_y{i}", [P, 2 * D]) for i in range(2)]
            ps_f = pb("ps_f", [P, FT * D])
            ps_fb = pb("ps_fb", [1, D])

            x_loaded = [sem(f"x_loaded{i}") for i in range(2)]
            h1_stored = [sem(f"h1_stored{i}") for i in range(2)]
            x2_stored = [sem(f"x2_stored{i}") for i in range(2)]
            x_st, x_mv, x_sd, x_rs, x_nm, x2_done = (sem("a_x2" + s) for s in ("st", "mv", "sd", "rs", "nm", ""))
            sd_done, rs_done, nm_done = (sem("a_" + s) for s in ("sd_done", "rs_done", "nm_done"))
            (x_hi, x_lo, tok_done, h_done, st_done, mv_done, u_done, ut_done, u_hi, u_lo, bu_ps, bu_done,
             scan_done, s_hi, s_lo, y_done, hb_done, h1_done) = (sem("a_" + s) for s in (
                 "x_hi", "x_lo", "tok_done", "h_done", "stats_done", "meanvar_done", "u_done",
                 "uT_done", "u_hi", "u_lo", "bu_ps", "bu_done", "scan_done", "s_hi", "s_lo", "y_done", "hb_done",
                 "h1_done"))
            w1_loaded, w2_loaded, fold_ps, fold_out, fb_ps, fb_out, fb_in = (sem(s) for s in (
                "w1_loaded", "w2_loaded", "fold_ps", "fold_out", "fold_bias_ps", "fold_bias_out",
                "fold_bias_loaded"))
            h1b_done = sem("a_h1b_done")
            blk = pa.enter_context(nc.Block())
            h1_grp, x2_grp = (t.rearrange("(g s p) d -> g p s d", s=2, p=P) for t in (h1_dram, x2_dram))

            @blk.sync
            def _(sp):
                def load(m):
                    wait(sp, x_hi, m.n() - 1)
                    wait(sp, x_lo, m.n() - 1)
                    sp.dma_start(xf[:, m.slot(2), :], xt[m.n()]).then_inc(x_loaded[m.slot(2)], 16)

                def store(m):
                    wait(sp, h1b_done, m.n() + 1)
                    sp.dma_start(h1_grp[m.n()], h1b[:, m.slot(2)]).then_inc(h1_stored[m.slot(2)], 16)
                    wait(sp, x2_done, m.n() * 2 + 2)
                    sp.dma_start(x2_grp[m.n()], x2o[:, m.slot(2)]).then_inc(x2_stored[m.slot(2)], 16)

                load(At(0, 0))
                load(At(0, 1))
                sp.dma_start(b12[:], b2c).then_inc(fb_in, 16)
                sp.dma_start(w1s[:], w1t[0]).then_inc(w1_loaded, 16)
                sp.dma_start(w2s[:], w2[0]).then_inc(w2_loaded, 16)
                load(At(0, 2))

                def next_expert(k):
                    if k.slot(FOLD) == 4:
                        wait(sp, fold_ps, k.turn(FOLD) + 1)
                        sp.dma_start(w1s[:], w1t[k.turn(FOLD) + 1]).then_inc(w1_loaded, 16)
                    elif k.slot(FOLD) == 5:
                        wait(sp, fb_ps, k.turn(FOLD) + 1)
                        sp.dma_start(w2s[:], w2[k.turn(FOLD) + 1]).then_inc(w2_loaded, 16)

                def step(k):
                    if k.valid(FOLD * (NE - 1)):
                        next_expert(k)
                    if k.back(-3).valid(NG):
                        load(k.back(-3))
                    if k.back(4).valid(NG):
                        store(k.back(4))

                run(sp, step, 0, NG + 4, 6, 42, FOLD)
                for i in range(2):
                    sp.wait_ge(h1_stored[i], 16 * ((NG + 1 - i) // 2))
                    sp.wait_ge(x2_stored[i], 16 * ((NG + 1 - i) // 2))

            @blk.scalar
            def _(act):
                def split_x(m):
                    p = m.slot(2)
                    wait(act, x_loaded[p], (m.turn(2) + 1) * 16)
                    wait(act, tok_done, m.n() * 2 - 2)
                    nc.scalar.activation(xh[:, p, :], xf[:, p, :], ACT.Copy).then_inc(x_hi, 1)

                def split_u(m):
                    wait(act, ut_done, m.n() + 1)
                    wait(act, y_done, m.n() - 1)
                    nc.scalar.activation(uh[:, m.slot(2), :], ps_t[:], ACT.Copy).then_inc(u_hi, 1)

                def inputs(m):
                    wait(act, bu_ps, m.n() + 1)
                    wait(act, scan_done, m.n() * 2 - 2)
                    for t in range(FT):
                        nc.scalar.activation(bu[:, m.slot(2), t, :], ps_b[:, t * G:(t + 1) * G], ACT.Identity,
                                             bias=c_bbdt[:, t:t + 1], scale=c_dt).then_inc(bu_done, 1)

                def split_s(m):
                    wait(act, scan_done, m.n() * 2 + 2)
                    wait(act, y_done, m.n() - 1)
                    nc.scalar.activation(sh[:, m.slot(2), :], xs[:, m.slot(2)].rearrange("p t g -> p (t g)"),
                                         ACT.Copy).then_inc(s_hi, 1)

                def dev_h(m, s):
                    wait(act, mv_done, m.n() * 2 + s + 1)
                    nc.scalar.activation(nrm[:, 0, s:s + 1], mv[:, s, 1:2], ACT.Sqrt, bias=c_eps[:]).then_inc(sd_done, 1)

                def norm_u(m, s):
                    p = m.slot(2)
                    wait(act, nm_done, m.n() * 2 + s + 1)
                    wait(act, ut_done, m.n() - 1)
                    nc.scalar.activation(u[:, p, s, :], h[:, p, s, :], ACT.Identity, bias=nrm[:, 2, s:s + 1],
                                         scale=nrm[:, 1, s:s + 1]).then_inc(u_done, 1)

                def dev_x(m):
                    wait(act, x_mv, m.n() * 2 + 2)
                    nc.scalar.activation(nrm_x[:, 0, :], mv_x[:, :, 1], ACT.Sqrt, bias=c_eps[:]).then_inc(x_sd, 1)

                def norm_x(m):
                    p = m.slot(2)
                    wait(act, x_nm, m.n() + 1)
                    wait(act, x2_stored[p], m.turn(2) * 16)
                    for s in range(2):
                        nc.scalar.activation(x2o[:, p, s, :], h1o[:, p, s, :], ACT.Identity, bias=nrm_x[:, 2, s:s + 1],
                                             scale=nrm_x[:, 1, s:s + 1]).then_inc(x2_done, 1)

                split_x(At(0, 0))
                split_x(At(0, 1))

                def step(k):
                    for m, stage in ((k.back(3), inputs), (k.back(4), dev_x), (k.back(3), split_s),
                                     (k.back(4), norm_x), (k, lambda m: dev_h(m, 0)), (k, lambda m: norm_u(m, 0)),
                                     (k, lambda m: dev_h(m, 1)), (k.back(-2), split_x),
                                     (k, lambda m: norm_u(m, 1)), (k.back(1), split_u)):
                        if m.valid(NG):
                            stage(m)
                    if k.slot(FOLD) == 3 and k.valid(FOLD * NE):
                        e = k.turn(FOLD)
                        wait(act, fold_ps, e + 1)
                        nc.scalar.activation(w12[:, bass.ds(e, 1), :].rearrange("p a d -> p (a d)"), ps_f[:],
                                             ACT.Copy).then_inc(fold_out, 1)

                run(act, step, 0, NG + 4, 6, 42, FOLD)

            @blk.gpsimd
            def _(pool):
                def split_x(m):
                    p = m.slot(2)
                    wait(pool, x_hi, m.n() + 1)
                    wait(pool, tok_done, m.n() * 2 - 2)
                    nc.gpsimd.tensor_tensor(xl[:, p, :], xf[:, p, :], xh[:, p, :].bitcast(F32),
                                            ALU.subtract).then_inc(x_lo, 1)

                def add_bias(m):
                    p = m.slot(2)
                    wait(pool, h_done, m.n() * 2 + 2)
                    wait(pool, h1_done, m.n() - 2)
                    nc.gpsimd.tensor_tensor(hb[:, m.slot(3)], h[:, p], r_bcd.unsqueeze(1).to_broadcast([P, 2, D]),
                                            ALU.add).then_inc(hb_done, 1)

                def add_out(m):
                    p = m.slot(2)
                    wait(pool, h1_done, m.n() + 1)
                    wait(pool, h1_stored[p], m.turn(2) * 16)
                    nc.gpsimd.tensor_tensor(h1b[:, p], h1o[:, p], r_be2.unsqueeze(1).to_broadcast([P, 2, D]),
                                            ALU.add).then_inc(h1b_done, 1)

                def step(k):
                    if k.valid(NG):
                        add_bias(k)
                    if k.back(-2).valid(NG):
                        split_x(k.back(-2))
                    if k.back(3).valid(NG):
                        add_out(k.back(3))

                split_x(At(0, 0))
                split_x(At(0, 1))
                run(pool, step, 0, NG + 3, 6, 42, FOLD)

            @blk.vector
            def _(dve):
                v = nc.vector

                def split_u(m):
                    p = m.slot(2)
                    wait(dve, u_hi, m.n() + 1)
                    wait(dve, y_done, m.n() - 1)
                    v.tensor_tensor(ul[:, p, :], ps_t[:], uh[:, p, :].bitcast(F32), ALU.subtract).then_inc(u_lo, 1)

                def scan(m, t):
                    p = m.slot(2)
                    wait(dve, bu_done, m.n() * 2 + 1 + t)
                    wait(dve, s_hi, m.n() - 1)
                    wait(dve, scan_done, m.n() * 2 - 1 + t)
                    first = isinstance(m.t, int) and m.c == 0
                    v.tensor_tensor_scan(xs[:, p, t, :], decay[:, t, bass.ds(m.n() * G % N, G)], bu[:, p, t, :],
                                         0.0 if first else xs[:, 1 - p, t, G - 1:G],
                                         ALU.mult, ALU.add).then_inc(scan_done, 1)

                def split_s(m):
                    p = m.slot(2)
                    wait(dve, s_hi, m.n() + 1)
                    wait(dve, y_done, m.n() - 1)
                    v.tensor_tensor(sl[:, p, :], xs[:, p].rearrange("p t g -> p (t g)"), sh[:, p, :].bitcast(F32),
                                    ALU.subtract).then_inc(s_lo, 1)

                def hidden(m, s):
                    p, n = m.slot(2), m.n() * 2 + s + 1
                    if s == 0:
                        wait(dve, hb_done, m.n() - 1)
                    wait(dve, u_done, m.n() * 2 - 2)
                    wait(dve, tok_done, n)
                    v.tensor_tensor(h[:, p, s, :], ps_h[s][:], r_btok, ALU.add).then_inc(h_done, 1)

                def stats_h(m, s):
                    wait(dve, h_done, m.n() * 2 + s + 1)
                    v.bn_stats(stats[:, s, :], h[:, m.slot(2), s, :]).then_inc(st_done, 1)

                def mean_h(m, s):
                    wait(dve, st_done, m.n() * 2 + s + 1)
                    wait(dve, u_done, m.n() * 2 - 2)
                    apart(dve, passed["dve"])
                    v.bn_aggr(mv[:, s, :], stats[:, s, :]).then_inc(mv_done, 1)

                def scale_h(m, s):
                    n = m.n() * 2 + s + 1
                    wait(dve, sd_done, n)
                    wait(dve, u_done, n - 2)
                    v.reciprocal(nrm[:, 1, s:s + 1], nrm[:, 0, s:s + 1]).then_inc(rs_done, 1)

                def shift_h(m, s):
                    wait(dve, rs_done, m.n() * 2 + s + 1)
                    v.scalar_tensor_tensor(nrm[:, 2, s:s + 1], mv[:, s, 0:1], -1.0, nrm[:, 1, s:s + 1], ALU.mult,
                                           ALU.mult).then_inc(nm_done, 1)

                def residual(m):
                    p = m.slot(2)
                    wait(dve, y_done, m.n() + 1)
                    wait(dve, hb_done, m.n() + 1)
                    wait(dve, h1b_done, m.n() - 1)
                    wait(dve, x2_done, m.n() * 2 - 2)
                    v.tensor_tensor(h1o[:, p], ps_y[p][:].rearrange("p (s d) -> p s d", s=2), hb[:, m.slot(3)],
                                    ALU.add).then_inc(h1_done, 1)

                def stats_x(m):
                    wait(dve, h1_done, m.n() + 1)
                    for s in range(2):
                        v.bn_stats(st_x[:, s, :], h1o[:, m.slot(2), s, :]).then_inc(x_st, 1)

                def mean_x(m):
                    wait(dve, x_st, m.n() * 2 + 2)
                    wait(dve, x2_done, m.n() * 2)
                    apart(dve, passed["dve"])
                    for s in range(2):
                        v.bn_aggr(mv_x[:, s, :], st_x[:, s, :]).then_inc(x_mv, 1)

                def scale_x(m):
                    wait(dve, x_sd, m.n() + 1)
                    v.reciprocal(nrm_x[:, 1, :], nrm_x[:, 0, :]).then_inc(x_rs, 1)

                def shift_x(m):
                    wait(dve, x_rs, m.n() + 1)
                    v.scalar_tensor_tensor(nrm_x[:, 2, :], mv_x[:, :, 0], -1.0, nrm_x[:, 1, :], ALU.mult,
                                           ALU.mult).then_inc(x_nm, 1)

                def fold_bias(k):
                    if k.slot(FOLD) == 5 and k.valid(FOLD * NE):
                        e = k.turn(FOLD)
                        wait(dve, fb_ps, e + 1)
                        if isinstance(k.t, int):
                            dve.wait_ge(fb_in, 16)
                        row = b12[0:1, bass.ds(e, 1), :].rearrange("p a d -> p (a d)")
                        v.tensor_tensor(row, ps_fb[:], row, ALU.add).then_inc(fb_out, 1)

                def of(stage, i):
                    return lambda m: stage(m, i)

                def step(k):
                    for m, stage in ((k.back(3), of(scan, 0)), (k.back(3), of(scan, 1)), (k.back(4), scale_x),
                                     (k, of(hidden, 0)), (k.back(4), shift_x), (k, of(stats_h, 0)),
                                     (k.back(3), split_s), (k, of(mean_h, 0)), (k, of(hidden, 1)),
                                     (k, of(scale_h, 0)), (k, of(stats_h, 1)), (k, of(shift_h, 0)),
                                     (k, of(mean_h, 1)), (k, of(scale_h, 1)), (k, of(shift_h, 1)),
                                     (k, fold_bias), (k.back(3), residual), (k.back(1), split_u),
                                     (k.back(3), stats_x), (k.back(3), mean_x)):
                        if m.valid(NG):
                            stage(m)

                run(dve, step, 0, NG + 4, 6, 42, FOLD)

            @blk.tensor
            def _(pe):
                def tokens(m, s):
                    p = m.slot(2)
                    if s == 0:
                        wait(pe, x_lo, m.n() + 1)
                    wait(pe, h_done, m.n() * 2 + s - 1)
                    last = product(ps_h[s][:],
                                   [(both(xh, xl, slice(None), p, slice(t * G + s * P, t * G + (s + 1) * P)),
                                     both(wh, wl, slice(None), slice(W_TOK + t * D, W_TOK + (t + 1) * D)))
                                    for t in range(KT)])
                    last.then_inc(tok_done, 1)

                def turn_u(m):
                    p = m.slot(2)
                    wait(pe, u_done, m.n() * 2 + 2)
                    wait(pe, u_lo, m.n())
                    for s in range(2):
                        for t in range(FT):
                            last = nc.tensor.transpose(ps_t[:, t * G + s * P:t * G + (s + 1) * P],
                                                       u[:, p, s, t * P:(t + 1) * P], ident[:])
                    last.then_inc(ut_done, 1)

                def inputs(m):
                    p = m.slot(2)
                    wait(pe, u_lo, m.n() + 1)
                    wait(pe, bu_done, m.n() * 2)
                    for o in range(FT):
                        last = product(ps_b[:, o * G:(o + 1) * G],
                                       [(both(wh, wl, slice(None), slice(W_B + t * D + o * P, W_B + t * D + (o + 1) * P)),
                                         both(uh, ul, slice(None), p, slice(t * G, (t + 1) * G))) for t in range(FT)])
                    last.then_inc(bu_ps, 1)

                def outputs(m):
                    p = m.slot(2)
                    wait(pe, s_lo, m.n() + 1)
                    wait(pe, h1_done, m.n() - 1)
                    for s in range(2):
                        last = product(ps_y[p][:, s * D:(s + 1) * D],
                                       [(both(a, b, slice(None), p, slice(t * G + s * P, t * G + (s + 1) * P)),
                                         both(wh, wl, slice(None), slice(w + t * D, w + (t + 1) * D)))
                                        for a, b, w in ((uh, ul, W_D), (sh, sl, W_C)) for t in range(FT)])
                    last.then_inc(y_done, 1)

                def fold(k):
                    e, c = k.turn(FOLD), k.slot(FOLD) // 2
                    if k.slot(FOLD) == 0:
                        wait(pe, w1_loaded, (e + 1) * 16)
                        wait(pe, w2_loaded, (e + 1) * 16)
                        wait(pe, fold_out, e)
                    if k.slot(FOLD) == 4:
                        wait(pe, fb_out, e)
                        if isinstance(k.t, int):
                            pe.wait_ge(fb_in, 16)
                    if k.slot(FOLD) in (0, 2):
                        for f in range(FK):
                            last = nc.tensor.matmul(ps_f[:, c * D:(c + 1) * D], w1s[:, f * D + c * P:f * D + (c + 1) * P],
                                                    w2s[:, f * D:(f + 1) * D], start=(f == 0), stop=(f == FK - 1))
                        if c == 1:
                            last.then_inc(fold_ps, 1)
                    if k.slot(FOLD) == 4:
                        for f in range(FK):
                            last = nc.tensor.matmul(ps_fb[:], w2s[:, FK * D + f:FK * D + f + 1], w2s[:, f * D:(f + 1) * D],
                                                    start=(f == 0), stop=(f == FK - 1))
                        last.then_inc(fb_ps, 1)

                def step(k):
                    if k.valid(NG):
                        tokens(k, 0)
                        tokens(k, 1)
                    if k.back(1).valid(NG):
                        turn_u(k.back(1))
                    if k.back(3).valid(NG):
                        outputs(k.back(3))
                    if k.valid(FOLD * NE):
                        fold(k)
                    if k.back(2).valid(NG):
                        inputs(k.back(2))

                run(pe, step, 0, NG + 3, 6, 48, FOLD)

        with ExitStack() as pb_:
            def pb(name, shape):
                return pb_.enter_context(nc.psum_tensor(name, shape, F32))

            x2 = sb("x2", [P, 2, 2, D], F32, pb_)
            x2b = sb("x2b", [P, 2, 2, D], F32, pb_)
            xh, xl = sb("x2h", [P, FT * G], F32R, pb_), sb("x2l", [P, FT * G], F32R, pb_)
            q, kk = sb("q", [P, FT * G], F32, pb_), sb("k", [P, FT * G], F32, pb_)
            va = sb("va", [P, 2, 2, H, HS], F32, pb_)
            ss = sb("ss", [P, 2 * H, L], F32, pb_)
            eb = sb("eb", [P, H * P], F32, pb_)
            et = sb("et", [P, H * P], F32, pb_)
            o = sb("o", [P, 2, H, HD], F32, pb_)
            oh_, ol_ = sb("oTh", [P, FT * G], F32R, pb_), sb("oTl", [P, FT * G], F32R, pb_)
            z = sb("z", [P, 2, D], F32, pb_)
            zg = sb("zg", [P, 2, D], F32, pb_)
            y1t = sb("y1t", [P, FT * G], F32, pb_)
            rows = sb("rows", [P, 2, 2, ROW], F32, pb_)
            mx = sb("mx", [P, 2 * H], F32, pb_)
            rinv = sb("rinv", [P, 2, H], F32, pb_)
            small = sb("small", [P, 16], F32, pb_)
            lmax, esum, cmax, slot_f = (small[:, i:i + 2] for i in (0, 2, 4, 6))
            slot_i = sb("slot_i", [P, 2, 2], I32, pb_)
            dl, el, cand, pos = (sb(s, [P, 2, NE], F32, pb_) for s in ("dl", "el", "cand", "pos"))
            oh = sb("oh", [P, 2, NE], BF16, pb_)
            zn = sb("zn", [P, 2, D], F32, pb_)
            st_z, mv_z = sb("st_z", [P, 2, 6], F32, pb_), sb("mv_z", [P, 2, 2], F32, pb_)
            ve_z, rs_z, nm_z = (sb(s, [P, 2], F32, pb_) for s in ("ve_z", "rs_z", "nm_z"))
            b_0, b_1, b_3, b_4 = (pb(f"b_{i}", [P, 512]) for i in (0, 1, 3, 4))
            ps_s = pb("ps_s", [P, 512])
            ps_o = pb("ps_o", [P, 2, 512])
            b_2 = ps_o[:, 1, :]
            ps_r = pb("ps_r", [P, 512])
            logit = ps_r[:, 0:2 * NE].rearrange("p (s e) -> p s e", s=2)
            order = ps_r[:, 256:256 + 2 * NE].rearrange("p (s e) -> p s e", s=2)

            x_loaded = [sem(f"b_x_loaded{i}") for i in range(2)]
            r_loaded = [sem(f"b_row_loaded{i}") for i in range(2)]
            scattered = [sem(f"b_scattered{i}") for i in range(2)]
            names = ("x2b x2T x2hi x2lo v_ps v_out q_ps q_out k_ps k_out s_ps max sub exp et_ps "
                     "et_out av_ps rinv o oT o_hi o_lo out_ps z zst zmv zve zrs znm zn zg y1 y1T_ps y1T logit_ps lmax "
                     "dlog elog esum gate cand cmax onehot acc order_ps pos posm slot slot_i ohcopy scopy ones").split()
            Q = {s: sem("b_" + s) for s in names}
            h1_tok, x2_tok = (a.rearrange("(l j s t) d -> t j l s d", l=L, j=NG, s=2, t=2) for a in (h1_dram, x2_dram))
            blk = pb_.enter_context(nc.Block())

            @blk.sync
            def _(sp):
                def load(m):
                    p = m.slot(2)
                    wait(sp, Q["x2T"], m.n() - 1)
                    wait(sp, Q["x2b"], m.n() - 1)
                    for t in range(2):
                        sp.dma_start(x2[t * L:(t + 1) * L, p], x2_tok[t, m.n()]).then_inc(x_loaded[p], 16)

                def load_row(m):
                    p = m.slot(2)
                    wait(sp, scattered[p], m.turn(2) * 32)
                    for t in range(2):
                        sp.dma_start(rows[t * L:(t + 1) * L, p, :, D:2 * D], h1_tok[t, m.n()]).then_inc(r_loaded[p], 16)

                load(At(0, 0))
                load(At(0, 1))

                def step(k):
                    if k.back(-2).valid(NG):
                        load(k.back(-2))
                    if k.back(2).valid(NG):
                        load_row(k.back(2))

                run(sp, step, 0, NG + 2, 6, 46)

            @blk.scalar
            def _(act):
                A = nc.scalar.activation

                def o_hi(m):
                    wait(act, Q["oT"], m.n() + 1)
                    wait(act, Q["out_ps"], m.n())
                    A(oh_[:], b_2, ACT.Copy).then_inc(Q["o_hi"], 1)

                def exps(m):
                    wait(act, Q["sub"], m.n() + 1)
                    wait(act, Q["et_ps"], m.n())
                    A(eb[:], ss[:].rearrange("p c m -> p (c m)"), ACT.Exp, scale=1.0 / float(HD) ** 0.5).then_inc(Q["exp"], 1)

                def v_out(m):
                    if isinstance(m.t, int) and m.c == 0:
                        act.wait_ge(Q["ones"], 1)
                    wait(act, Q["v_ps"], m.n() + 1)
                    wait(act, Q["av_ps"], m.n() - 1)
                    A(va[:, m.slot(2), :, :, 0:HD], b_3[:].rearrange("p (s h d) -> p s h d", s=2, h=H),
                      ACT.Copy).then_inc(Q["v_out"], 1)

                def qk_out(m, ps, dst, at, done):
                    wait(act, Q[ps], m.n() + 1)
                    wait(act, Q["s_ps"], m.n())
                    src = b_1 if ps == "q_ps" else b_4
                    for t in range(FT):
                        A(dst[:, t * G:(t + 1) * G], src[:, t * G:(t + 1) * G], ACT.Identity,
                          bias=c_bqk[:, at + t:at + t + 1]).then_inc(Q[done], 1)

                def e_log(m):
                    wait(act, Q["dlog"], m.n() + 1)
                    A(el[:], dl[:], ACT.Exp).then_inc(Q["elog"], 1)

                def et_out(m):
                    wait(act, Q["et_ps"], m.n() + 1)
                    wait(act, Q["av_ps"], m.n())
                    A(et[:], b_1[:], ACT.Copy).then_inc(Q["et_out"], 1)

                def z_norm(m):
                    wait(act, Q["znm"], m.n() + 1)
                    wait(act, Q["zg"], m.n())
                    for s in range(2):
                        A(zn[:, s, :], z[:, s, :], ACT.Identity, bias=nm_z[:, s:s + 1],
                          scale=rs_z[:, s:s + 1]).then_inc(Q["zn"], 1)

                def x_hi(m):
                    wait(act, Q["x2T"], m.n() + 1)
                    A(xh[:], b_2, ACT.Copy).then_inc(Q["x2hi"], 1)

                def y1t_out(m):
                    wait(act, Q["y1T_ps"], m.n() + 1)
                    wait(act, Q["logit_ps"], m.n())
                    A(y1t[:], b_0[:], ACT.Copy).then_inc(Q["y1T"], 1)

                def step(k):
                    for m, stage in ((k.back(3), z_norm), (k.back(2), o_hi), (k.back(1), exps), (k, v_out),
                                     (k, lambda m: qk_out(m, "q_ps", q, 0, "q_out")),
                                     (k.back(3), y1t_out), (k, lambda m: qk_out(m, "k_ps", kk, FT, "k_out")),
                                     (k.back(-1), x_hi), (k.back(1), et_out), (k.back(3), e_log)):
                        if m.valid(NG):
                            stage(m)

                run(act, step, -1, NG + 4, 6, 48)

            @blk.gpsimd
            def _(pool):
                g = nc.gpsimd
                g.memset(va[:], 1.0).then_inc(Q["ones"], 1)

                def rstd(m):
                    wait(pool, Q["zmv"], m.n() * 2 + 2)
                    wait(pool, Q["zn"], m.n() * 2)
                    apart(pool, passed["pool"])
                    g.tensor_scalar(ve_z[:], mv_z[:, :, 1], EPS, None, ALU.add).then_inc(Q["zve"], 1)
                    wait(pool, Q["zve"], m.n() + 1)
                    g.tensor_tensor(rs_z[:], ve_z[:], mhalf[:], ALU.pow).then_inc(Q["zrs"], 1)

                def add_bias(m):
                    p = m.slot(2)
                    wait(pool, x_loaded[p], (m.turn(2) + 1) * 32)
                    wait(pool, Q["z"], m.n() - 1)
                    g.tensor_tensor(x2b[:, p], x2[:, p], r_bo.unsqueeze(1).to_broadcast([P, 2, D]),
                                    ALU.add).then_inc(Q["x2b"], 1)

                def count(m):
                    wait(pool, Q["order_ps"], m.n() + 1)
                    for s in range(2):
                        wait(pool, Q["acc"], m.n() * 2 + s)
                        g.tensor_tensor(oh_acc[:], oh_acc[:], oh[:, s, :], ALU.add).then_inc(Q["acc"], 1)
                    g.tensor_copy(oh_all[:, bass.ds(m.n() * 2, 2), :], oh[:]).then_inc(Q["ohcopy"], 1)

                def send(m):
                    p = m.slot(2)
                    wait(pool, r_loaded[p], (m.turn(2) + 1) * 32)
                    apart(pool, passed["pool"])
                    g.tensor_copy(rows[:, p, :, OFF_S], s_tab[:, bass.ds(m.n() * 2, 2)]).then_inc(Q["scopy"], 1)
                    wait(pool, Q["slot"], m.n() + 1)
                    apart(pool, passed["pool"])
                    g.tensor_copy(slot_i[:, p, :], slot_f).then_inc(Q["slot_i"], 1)
                    wait(pool, Q["slot_i"], m.n() + 1)
                    wait(pool, Q["scopy"], m.n() + 1)
                    wait(pool, Q["gate"], m.n() + 1)
                    apart(pool, passed["pool"])
                    for s in range(2):
                        g.indirect_dma_start(bins, bass.IndirectOffsetOnAxis(ap=slot_i[:, p, s:s + 1], axis=0),
                                             rows[:, p, s, :], None).then_inc(scattered[p], 16)

                def step(k):
                    for m, stage in ((k.back(4), count), (k.back(4), send), (k, add_bias), (k.back(2), rstd)):
                        if m.valid(NG):
                            stage(m)

                run(pool, step, 0, NG + 4, 6, 48)
                for i in range(2):
                    pool.wait_ge(scattered[i], 32 * ((NG + 1 - i) // 2))

            @blk.vector
            def _(dve):
                v = nc.vector

                def x_lo(m):
                    wait(dve, Q["x2hi"], m.n() + 1)
                    v.tensor_tensor(xl[:], b_2, xh[:].bitcast(F32), ALU.subtract).then_inc(Q["x2lo"], 1)

                def o_lo(m):
                    wait(dve, Q["o_hi"], m.n() + 1)
                    wait(dve, Q["out_ps"], m.n())
                    v.tensor_tensor(ol_[:], b_2, oh_[:].bitcast(F32), ALU.subtract).then_inc(Q["o_lo"], 1)

                def softmax(m):
                    wait(dve, Q["s_ps"], m.n() + 1)
                    wait(dve, Q["exp"], m.n())
                    sv = ps_s[:].rearrange("p (c m) -> p c m", m=L)
                    v.tensor_reduce(mx[:], sv, AX_X, ALU.max).then_inc(Q["max"], 1)
                    wait(dve, Q["max"], m.n() + 1)
                    v.tensor_tensor(ss[:], sv, mx[:].unsqueeze(2).to_broadcast([P, 2 * H, L]),
                                    ALU.subtract).then_inc(Q["sub"], 1)

                def o_norm(m):
                    wait(dve, Q["av_ps"], m.n() + 1)
                    wait(dve, Q["oT"], m.n())
                    av = ps_o[:, :, 0:H * HS].rearrange("p s (h d) -> p s h d", h=H)
                    v.reciprocal(rinv[:], av[:, :, :, HD]).then_inc(Q["rinv"], 1)
                    wait(dve, Q["rinv"], m.n() + 1)
                    v.tensor_tensor(o[:], av[:, :, :, 0:HD], rinv[:].unsqueeze(3).to_broadcast([P, 2, H, HD]),
                                    ALU.mult).then_inc(Q["o"], 1)

                def residual(m):
                    p = m.slot(2)
                    wait(dve, Q["out_ps"], m.n() + 1)
                    wait(dve, Q["x2b"], m.n() + 1)
                    wait(dve, Q["zn"], m.n() * 2)
                    v.tensor_tensor(z[:], b_0[:].rearrange("p (s d) -> p s d", s=2), x2b[:, p], ALU.add).then_inc(Q["z"], 1)
                    wait(dve, Q["z"], m.n() + 1)
                    for s in range(2):
                        v.bn_stats(st_z[:, s, :], z[:, s, :]).then_inc(Q["zst"], 1)

                def mean(m):
                    wait(dve, Q["zst"], m.n() * 2 + 2)
                    wait(dve, Q["znm"], m.n())
                    apart(dve, passed["dve"])
                    for s in range(2):
                        v.bn_aggr(mv_z[:, s, :], st_z[:, s, :]).then_inc(Q["zmv"], 1)

                def shift(m):
                    wait(dve, Q["zrs"], m.n() + 1)
                    v.scalar_tensor_tensor(nm_z[:], mv_z[:, :, 0], -1.0, rs_z[:], ALU.mult, ALU.mult).then_inc(Q["znm"], 1)

                def y1(m):
                    p = m.slot(2)
                    wait(dve, Q["zn"], m.n() * 2 + 2)
                    wait(dve, scattered[p], m.turn(2) * 32)
                    v.tensor_tensor(zg[:], zn[:], r_g1.unsqueeze(1).to_broadcast([P, 2, D]), ALU.mult).then_inc(Q["zg"], 1)
                    wait(dve, Q["zg"], m.n() + 1)
                    v.tensor_tensor(rows[:, p, :, 0:D], zg[:], r_be1.unsqueeze(1).to_broadcast([P, 2, D]),
                                    ALU.add).then_inc(Q["y1"], 1)

                def top_logit(m):
                    wait(dve, Q["logit_ps"], m.n() + 1)
                    v.tensor_reduce(lmax, logit, AX_X, ALU.max).then_inc(Q["lmax"], 1)

                def expert(m):
                    wait(dve, Q["lmax"], m.n() + 1)
                    v.tensor_tensor(dl[:], logit, lmax.unsqueeze(2).to_broadcast([P, 2, NE]),
                                    ALU.subtract).then_inc(Q["dlog"], 1)
                    wait(dve, Q["dlog"], m.n() + 1)
                    v.scalar_tensor_tensor(cand[:], dl[:], 0.0, rank8[:].unsqueeze(1).to_broadcast([P, 2, NE]),
                                           ALU.is_ge, ALU.mult).then_inc(Q["cand"], 1)
                    wait(dve, Q["cand"], m.n() + 1)
                    v.tensor_reduce(cmax, cand[:], AX_X, ALU.max).then_inc(Q["cmax"], 1)
                    wait(dve, Q["cmax"], m.n() + 1)
                    wait(dve, Q["ohcopy"], m.n())
                    wait(dve, Q["posm"], m.n())
                    v.tensor_tensor(oh[:], cand[:], cmax.unsqueeze(2).to_broadcast([P, 2, NE]),
                                    ALU.is_equal).then_inc(Q["onehot"], 1)

                def gates(m):
                    p = m.slot(2)
                    wait(dve, Q["elog"], m.n() + 1)
                    v.tensor_reduce(esum, el[:], AX_X, ALU.add).then_inc(Q["esum"], 1)
                    wait(dve, Q["esum"], m.n() + 1)
                    v.reciprocal(rows[:, p, :, OFF_GATE], esum).then_inc(Q["gate"], 1)

                def place(m):
                    wait(dve, Q["order_ps"], m.n() + 1)
                    v.tensor_tensor(pos[:], order, ebase[:].unsqueeze(1).to_broadcast([P, 2, NE]),
                                    ALU.add).then_inc(Q["pos"], 1)
                    wait(dve, Q["pos"], m.n() + 1)
                    v.tensor_tensor(pos[:], pos[:], oh[:], ALU.mult).then_inc(Q["posm"], 1)
                    wait(dve, Q["posm"], m.n() + 1)
                    wait(dve, Q["slot_i"], m.n())
                    v.tensor_reduce(slot_f, pos[:], AX_X, ALU.add).then_inc(Q["slot"], 1)

                def step(k):
                    for m, stage in ((k.back(2), o_norm), (k.back(3), shift), (k.back(1), softmax), (k.back(3), y1),
                                     (k.back(2), o_lo), (k.back(4), place), (k.back(-1), x_lo),
                                     (k.back(3), top_logit), (k.back(3), expert), (k.back(2), residual),
                                     (k.back(3), gates), (k.back(2), mean)):
                        if m.valid(NG):
                            stage(m)

                run(dve, step, -1, NG + 4, 6, 48)

            @blk.tensor
            def _(pe):
                mm = nc.tensor.matmul

                def turn(dst, src, at):
                    for s in range(2):
                        for t in range(FT):
                            last = nc.tensor.transpose(dst[:, t * G + s * P:t * G + (s + 1) * P], src(s, t), ident[:])
                    return last

                def values(m):
                    wait(pe, Q["x2lo"], m.n() + 1)
                    wait(pe, Q["v_out"], m.n())
                    for s in range(2):
                        last = product(b_3[:, s * D:(s + 1) * D],
                                       [(both(xh, xl, slice(None), slice(t * G + s * P, t * G + (s + 1) * P)),
                                         both(wh, wl, slice(None), slice(W_QKV + t * 3 * D + 2 * D, W_QKV + (t + 1) * 3 * D)))
                                        for t in range(FT)])
                    last.then_inc(Q["v_ps"], 1)

                def heads(m, dst, at, done):
                    for c in range(FT):
                        last = product(dst[:, c * G:(c + 1) * G],
                                       [(both(wh, wl, slice(None), slice(W_QKV + t * 3 * D + at + c * P,
                                                                         W_QKV + t * 3 * D + at + (c + 1) * P)),
                                         both(xh, xl, slice(None), slice(t * G, (t + 1) * G))) for t in range(FT)])
                    last.then_inc(Q[done], 1)

                def queries(m):
                    wait(pe, Q["et_out"], m.n() - 1)
                    heads(m, b_1, 0, "q_ps")

                def keys(m):
                    wait(pe, Q["k_out"], m.n() * 2)
                    heads(m, b_4, D, "k_ps")

                def gate(m):
                    wait(pe, Q["y1T"], m.n() + 1)
                    wait(pe, Q["pos"], m.n())
                    for s in range(2):
                        for t in range(FT):
                            last = mm(logit[:, s, :], y1t[:, t * G + s * P:t * G + (s + 1) * P], wg_sb[:, t, :],
                                      start=(t == 0), stop=(t == FT - 1))
                    last.then_inc(Q["logit_ps"], 1)

                def project(m):
                    wait(pe, Q["o_lo"], m.n() + 1)
                    wait(pe, Q["y1T"], m.n())
                    wait(pe, Q["z"], m.n())
                    for s in range(2):
                        last = product(b_0[:, s * D:(s + 1) * D],
                                       [(both(oh_, ol_, slice(None), slice(t * G + s * P, t * G + (s + 1) * P)),
                                         both(wh, wl, slice(None), slice(W_OUT + t * D, W_OUT + (t + 1) * D)))
                                        for t in range(FT)])
                    last.then_inc(Q["out_ps"], 1)

                def turn_e(m):
                    wait(pe, Q["exp"], m.n() + 1)
                    wait(pe, Q["q_out"], m.n() * 2 + 4, 2 * NG)
                    for c in range(H):
                        last = nc.tensor.transpose(b_1[:, c * P:(c + 1) * P], eb[:, c * P:(c + 1) * P], ident[:])
                    last.then_inc(Q["et_ps"], 1)

                def turn_x(m):
                    p = m.slot(2)
                    wait(pe, x_loaded[p], (m.turn(2) + 1) * 32)
                    wait(pe, Q["o_lo"], m.n() - 2)
                    turn(b_2, lambda s, t: x2[:, p, s, t * P:(t + 1) * P], 0).then_inc(Q["x2T"], 1)

                def scores(m):
                    wait(pe, Q["q_out"], m.n() * 2 + 2)
                    wait(pe, Q["k_out"], m.n() * 2 + 2)
                    wait(pe, Q["sub"], m.n())
                    apart(pe, passed["pe"])
                    for s in range(2):
                        for t in range(2):
                            for hh in range(H):
                                b, a = hh // 2, hh % 2
                                r, c = slice(a * HD, (a + 1) * HD), slice(b * G + s * P + t * L, b * G + s * P + (t + 1) * L)
                                to = (s * 2 + b) * P + t * L
                                last = mm(ps_s[a * L:(a + 1) * L, to:to + L], q[r, c], kk[r, c], start=True, stop=True)
                    last.then_inc(Q["s_ps"], 1)

                def rank(m):
                    wait(pe, Q["onehot"], m.n() + 1)
                    wait(pe, Q["dlog"], m.n() + 1)
                    wait(pe, Q["acc"], m.n() * 2)
                    mm(order[:, 0, :], before[:], oh[:, 0, :], start=True, stop=False)
                    mm(order[:, 0, :], ones_b[:], oh_acc[:], start=False, stop=True)
                    mm(order[:, 1, :], before[:], oh[:, 1, :], start=True, stop=False)
                    mm(order[:, 1, :], ones_b[:], oh[:, 0, :], start=False, stop=False)
                    mm(order[:, 1, :], ones_b[:], oh_acc[:], start=False, stop=True).then_inc(Q["order_ps"], 1)

                def attend(m):
                    wait(pe, Q["et_out"], m.n() + 1)
                    wait(pe, Q["v_out"], m.n() + 1)
                    wait(pe, Q["o"], m.n())
                    wait(pe, Q["x2lo"], m.n() + 3, NG)
                    apart(pe, passed["pe"])
                    p = m.slot(2)
                    for s in range(2):
                        for t in range(2):
                            for hh in range(H):
                                r, c = slice(t * L, (t + 1) * L), (s * 2 + hh // 2) * P + (hh % 2) * L
                                last = mm(ps_o[r, s, hh * HS:(hh + 1) * HS], et[r, c:c + L], va[r, p, s, hh, :],
                                          start=True, stop=True)
                    last.then_inc(Q["av_ps"], 1)

                def turn_y(m):
                    wait(pe, Q["y1"], m.n() + 1)
                    wait(pe, Q["z"], m.n() + 1)
                    p = m.slot(2)
                    turn(b_0, lambda s, t: rows[:, p, s, t * P:(t + 1) * P], 0).then_inc(Q["y1T_ps"], 1)

                def turn_o(m):
                    wait(pe, Q["o"], m.n() + 1)
                    of = o[:].rearrange("p s h d -> p s (h d)")
                    turn(b_2, lambda s, t: of[:, s, t * P:(t + 1) * P], 0).then_inc(Q["oT"], 1)

                def step(k):
                    for m, stage in ((k, values), (k.back(2), turn_o), (k, queries), (k, keys), (k.back(3), turn_y),
                                     (k.back(-1), turn_x), (k.back(1), turn_e), (k.back(3), gate),
                                     (k.back(2), project), (k, scores), (k.back(1), attend), (k.back(3), rank)):
                        if m.valid(NG):
                            stage(m)

                run(pe, step, -1, NG + 4, 6, 48)

        with ExitStack() as pc:
            def pb(name, shape):
                return pc.enter_context(nc.psum_tensor(name, shape, F32))

            J = 2 * NG
            oht = sb("oht", [P, NE, J], F32, pc)
            cinc = sb("cinc", [P, NE, J], F32, pc)
            cexc = sb("cexc", [P, NE, J], F32, pc)
            tot = sb("tot", [P, NE, J], F32, pc)
            ones_j = sb("ones_j", [P, J], F32, pc)
            s1 = sb("s1", [P, J], F32, pc)
            kmax = sb("kmax", [P, NE], F32, pc)
            thr = sb("thr", [P, NE], F32, pc)
            cnt = sb("cnt", [P, NE], F32, pc)
            ci = sb("ci", [P, NE], I32, pc)
            fi = sb("fi", [P, NE], I32, pc)
            nt = sb("nt", [P, 4, NE], F32, pc)
            nti = sb("nti", [P, NE], I32, pc)
            one8 = sb("one8", [P, NE], F32, pc)
            tix_i, tix = sb("tix_i", [P, TILES], I32, pc), sb("tix", [P, TILES], F32, pc)
            ge, gw = sb("ge", [P, TILES, NE], F32, pc), sb("gw", [P, TILES, NE], F32, pc)
            tile_e, tile_r = sb("tile_e", [P, TILES], F32, pc), sb("tile_r", [P, TILES], F32, pc)
            tab_e, tab_r = sb("tab_e", [P, TILES], I32, pc), sb("tab_r", [P, TILES], I32, pc)
            row = sb("row", [P, 6, ROW], F32, pc)
            yt = sb("yt", [P, 2, FT * P], F32, pc)
            sidx = sb("sidx", [P, 6], I32, pc)
            thr_w, tile_thr = sb("thr_w", [P, TILES, NE], F32, pc), sb("tile_thr", [P, TILES], F32, pc)
            dthr = sb("dthr", [P, NE], F32, pc)
            gk = sb("gk", [P, 2], F32, pc)
            z = sb("c_z", [P, 2, D], F32, pc)
            st, mv = sb("c_st", [P, 2, 6], F32, pc), sb("c_mv", [P, 2, 2], F32, pc)
            ve, rs = sb("c_ve", [P, 2], F32, pc), sb("c_rs", [P, 2], F32, pc)
            zg = sb("c_zg", [P, 2, D], F32, pc)
            res = sb("res", [P, 6, D], F32, pc)
            ps_l = [pb(f"ps_l{i}", [P, 4, J]) for i in range(2)]
            ps_c = pb("ps_c", [P, NE])
            ps_t = [pb(f"c_ps_t{i}", [P, FT * P]) for i in range(2)]
            ps_y = [pb(f"c_ps_y{i}", [P, D]) for i in range(2)]

            own, cnt_ps, cexc_ready, loc_ps = (sem("c_" + s) for s in ("own", "count_ps", "ranks_in", "rank_ps"))
            kmax_ready, thr_ready, tab_ready, filled, tiota, fi_ready = (
                sem("c_" + s) for s in ("kmax", "threshold", "tables", "filled", "tile_iota", "fill_rows"))
            loaded = [sem(f"c_loaded{i}") for i in range(6)]
            sent = [sem(f"c_sent{i}") for i in range(6)]
            (yt_ps, yt_out, mm_ps, gk_s, z_s, st_s, mv_s, ve_s, rs_s, zg_s, res_s, idx_s) = (
                sem("c_" + s) for s in ("yT_ps", "yT", "expert_ps", "gk", "z", "st", "mv", "ve", "rs", "zg",
                                        "res", "idx"))
            blk = pc.enter_context(nc.Block())

            @blk.sync
            def _(sp):
                sp.dma_start(bins[BINS:BINS + P, :], fill[:]).then_inc(filled, 16)
                sp.wait_ge(fi_ready, 1)
                for e in range(NE):
                    r = sp.value_load(fi[0:1, e:e + 1], min_val=0, max_val=BINS)
                    sp.dma_start(bins[bass.ds(r, P), :], fill[:]).then_inc(filled, 16)
                sp.wait_ge(filled, 16 * (NE + 1))
                sp.wait_ge(tab_ready, 1)

                def load(k):
                    r = sp.value_load(tab_r[0:1, bass.ds(k.n(), 1)], min_val=0, max_val=BINS)
                    wait(sp, res_s, k.n() - 5)
                    wait(sp, idx_s, k.n() - 5)
                    sp.dma_start(row[:, k.slot(6), :], bins[bass.ds(r, P), :]).then_inc(loaded[k.slot(6)], 16)

                run(sp, load, 0, TILES, 12, TILES - 6, 6)

            @blk.scalar
            def _(act):
                def y_out(k):
                    wait(act, yt_ps, k.n() + 1)
                    wait(act, mm_ps, k.n() - 1)
                    nc.scalar.activation(yt[:, k.slot(2), :], ps_t[k.slot(2)][:], ACT.Copy).then_inc(yt_out, 1)

                def dev(k):
                    p = k.slot(2)
                    wait(act, mv_s, k.n() + 1)
                    wait(act, rs_s, k.n() - 1)
                    nc.scalar.activation(ve[:, p:p + 1], mv[:, p, 1:2], ACT.Sqrt, bias=c_eps[:]).then_inc(ve_s, 1)

                def step(k):
                    for m, stage in ((k, y_out), (k.back(1), dev)):
                        if m.valid(TILES):
                            stage(m)

                run(act, step, 0, TILES + 1, 12, TILES - 6, 6)

            @blk.gpsimd
            def _(pool):
                g = nc.gpsimd
                g.iota(tix_i[:], [[1, TILES]], base=0, channel_multiplier=0).then_inc(tiota, 1)
                pool.wait_ge(kmax_ready, 1)
                g.partition_all_reduce(thr[:], kmax[:], P, bass.bass_isa.ReduceOp.max).then_inc(thr_ready, 1)

                def send(k):
                    b = k.slot(6)
                    wait(pool, loaded[b], (k.turn(6) + 1) * 16)
                    wait(pool, sent[b], k.turn(6) * 16)
                    apart(pool, passed["pool"])
                    g.tensor_copy(sidx[:, b:b + 1], row[:, b, OFF_S:OFF_S + 1]).then_inc(idx_s, 1)
                    wait(pool, res_s, k.n() + 1)
                    wait(pool, idx_s, k.n() + 1)
                    apart(pool, passed["pool"])
                    g.indirect_dma_start(out, bass.IndirectOffsetOnAxis(ap=sidx[:, b:b + 1], axis=0), res[:, b, :],
                                         None, bounds_check=S - 1, oob_is_err=False).then_inc(sent[b], 16)

                run(pool, send, 0, TILES, 12, TILES - 6, 6)
                for i in range(6):
                    pool.wait_ge(sent[i], 16 * (TILES // 6))

            @blk.vector
            def _(dve):
                v = nc.vector
                count = [0]

                def link(ins):
                    count[0] += 1
                    ins.then_inc(own, 1)
                    dve.wait_ge(own, count[0])

                dve.wait_ge(cnt_ps, 1)
                link(v.tensor_copy(cnt[:], ps_c[:]))
                link(v.tensor_tensor(nt[:, 0, :], cnt[:], ebase[:], ALU.add))
                v.tensor_copy(fi[:], nt[:, 0, :]).then_inc(fi_ready, 1)
                link(v.tensor_scalar(cnt[:], cnt[:], float(P - 1), None, ALU.add))
                link(v.tensor_copy(ci[:], cnt[:]))
                link(v.tensor_scalar(nti[:], ci[:], 7, None, ALU.arith_shift_right))
                link(v.tensor_copy(nt[:, 1, :], nti[:]))
                link(v.memset(one8[:], 1.0))
                link(v.tensor_tensor_scan(nt[:, 2, :], one8[:], nt[:, 1, :], 0.0, ALU.mult, ALU.add))
                link(v.tensor_scalar(nt[:, 3, :], nt[:, 1, :], -float(P), float(BIN), ALU.mult, ALU.add))
                dve.wait_ge(tiota, 1)
                link(v.tensor_copy(tix[:], tix_i[:]))
                link(v.tensor_tensor(ge[:], tix[:].unsqueeze(2).to_broadcast([P, TILES, NE]),
                                     nt[:, 2, :].unsqueeze(1).to_broadcast([P, TILES, NE]), ALU.is_ge))
                link(v.tensor_tensor(gw[:], ge[:], nt[:, 3, :].unsqueeze(1).to_broadcast([P, TILES, NE]), ALU.mult))
                link(v.tensor_reduce(tile_e[:], ge[:], AX_X, ALU.add))
                link(v.tensor_reduce(tile_r[:], gw[:], AX_X, ALU.add))
                link(v.tensor_scalar(tix[:], tix[:], float(P), None, ALU.mult))
                link(v.tensor_tensor(tile_r[:], tile_r[:], tix[:], ALU.add))
                link(v.tensor_scalar(tab_r[:], tile_r[:], float(BINS), None, ALU.min))
                v.tensor_scalar(tab_e[:], tile_e[:], float(NE - 1), None, ALU.min).then_inc(tab_ready, 1)
                link(v.memset(ones_j[:], 1.0))
                link(v.tensor_copy(oht[:], oh_all[:].rearrange("p j e -> p e j")))
                for e in range(NE):
                    last = v.tensor_tensor_scan(cinc[:, e, :], ones_j[:], oht[:, e, :], 0.0, ALU.mult, ALU.add)
                link(last)
                link(v.tensor_tensor(cexc[:], cinc[:], oht[:], ALU.subtract))
                v.tensor_copy(tot[:], cinc[:, :, J - 1:J].to_broadcast([P, NE, J])).then_inc(cexc_ready, 1)
                link(v.tensor_scalar(s1[:], s_tab[:], 1.0, None, ALU.add))
                dve.wait_ge(loc_ps, 1)
                for i in range(2):
                    link(v.scalar_tensor_tensor(cexc[:, 4 * i:4 * i + 4, :], ps_l[i][:], float(CAP),
                                                oht[:, 4 * i:4 * i + 4, :], ALU.is_lt, ALU.mult))
                link(v.tensor_tensor(cexc[:], cexc[:], s1[:].unsqueeze(1).to_broadcast([P, NE, J]), ALU.mult))
                v.tensor_reduce(kmax[:], cexc[:], AX_X, ALU.max).then_inc(kmax_ready, 1)
                dve.wait_ge(thr_ready, 1)
                link(v.memset(dthr[:], 0.0))
                link(v.tensor_tensor(dthr[:, 0:NE - 1], thr[:, 1:NE], thr[:, 0:NE - 1], ALU.subtract))
                link(v.tensor_tensor(thr_w[:], ge[:], dthr[:].unsqueeze(1).to_broadcast([P, TILES, NE]), ALU.mult))
                link(v.tensor_reduce(tile_thr[:], thr_w[:], AX_X, ALU.add))
                link(v.tensor_scalar(tile_thr[:], tile_thr[:], thr[:, 0:1], None, ALU.add))

                def keep(k):
                    b, p = k.slot(6), k.slot(2)
                    wait(dve, loaded[b], (k.turn(6) + 1) * 16)
                    wait(dve, z_s, k.n() - 1)
                    v.tensor_scalar(gk[:, p:p + 1], row[:, b, OFF_S:OFF_S + 1], tile_thr[:, bass.ds(k.n(), 1)],
                                    row[:, b, OFF_GATE:OFF_GATE + 1], ALU.is_lt, ALU.mult).then_inc(gk_s, 1)

                def residual(k):
                    p = k.slot(2)
                    wait(dve, mm_ps, k.n() + 1)
                    wait(dve, gk_s, k.n() + 1)
                    wait(dve, zg_s, k.n() - 1)
                    v.scalar_tensor_tensor(z[:, p, :], ps_y[p][:], gk[:, p:p + 1], row[:, k.slot(6), 0:D], ALU.mult,
                                           ALU.add).then_inc(z_s, 1)

                def stats(k):
                    wait(dve, z_s, k.n() + 1)
                    v.bn_stats(st[:, k.slot(2), :], z[:, k.slot(2), :]).then_inc(st_s, 1)

                def mean(k):
                    wait(dve, st_s, k.n() + 1)
                    wait(dve, ve_s, k.n() - 1)
                    apart(dve, passed["dve"])
                    v.bn_aggr(mv[:, k.slot(2), :], st[:, k.slot(2), :]).then_inc(mv_s, 1)

                def scale(k):
                    p = k.slot(2)
                    wait(dve, ve_s, k.n() + 1)
                    v.reciprocal(rs[:, p:p + 1], ve[:, p:p + 1]).then_inc(rs_s, 1)

                def centre(k):
                    p = k.slot(2)
                    wait(dve, mv_s, k.n() + 1)
                    wait(dve, res_s, k.n() - 1)
                    v.scalar_tensor_tensor(zg[:, p, :], z[:, p, :], mv[:, p, 0:1], r_g2, ALU.subtract,
                                           ALU.mult).then_inc(zg_s, 1)

                def finish(k):
                    b, p = k.slot(6), k.slot(2)
                    wait(dve, zg_s, k.n() + 1)
                    wait(dve, rs_s, k.n() + 1)
                    wait(dve, sent[b], k.turn(6) * 16)
                    v.scalar_tensor_tensor(res[:, b, :], zg[:, p, :], rs[:, p:p + 1], row[:, b, D:2 * D], ALU.mult,
                                           ALU.add).then_inc(res_s, 1)

                def step(k):
                    for m, stage in ((k, keep), (k.back(1), centre), (k, residual), (k.back(1), scale), (k, stats),
                                     (k.back(1), finish), (k, mean)):
                        if m.valid(TILES):
                            stage(m)

                run(dve, step, 0, TILES + 1, 12, TILES - 6, 6)

            @blk.tensor
            def _(pe):
                mm = nc.tensor.matmul
                mm(ps_c[:], ones_b[:], oh_acc[:], start=True, stop=True).then_inc(cnt_ps, 1)
                pe.wait_ge(cexc_ready, 1)
                for i in range(2):
                    for c in range(4):
                        e = 4 * i + c
                        mm(ps_l[i][:, c, :], later_l[:], tot[:, e, :], start=True, stop=False)
                        mm(ps_l[i][:, c, :], same_l[:], cexc[:, e, :], start=False, stop=False)
                        last = mm(ps_l[i][:, c, :], first_n[:], oht[:, e, :], start=False, stop=True)
                last.then_inc(loc_ps, 1)
                pe.wait_ge(tab_ready, 1)

                def turn_y(k):
                    b = k.slot(6)
                    wait(pe, loaded[b], (k.turn(6) + 1) * 16)
                    wait(pe, yt_out, k.n() - 1)
                    for t in range(FT):
                        last = nc.tensor.transpose(ps_t[k.slot(2)][:, t * P:(t + 1) * P], row[:, b, t * P:(t + 1) * P],
                                                   ident[:])
                    last.then_inc(yt_ps, 1)

                def expert(k):
                    e = pe.value_load(tab_e[0:1, bass.ds(k.n(), 1)], min_val=0, max_val=NE - 1)
                    p = k.slot(2)
                    wait(pe, yt_out, k.n() + 1)
                    wait(pe, z_s, k.n() - 1)
                    for t in range(FT):
                        mm(ps_y[p][:], yt[:, p, t * P:(t + 1) * P],
                                  w12[:, bass.ds(e, 1), t * D:(t + 1) * D].rearrange("p a d -> p (a d)"),
                                  start=(t == 0), stop=False)
                    mm(ps_y[p][:], one_row[:], b12[0:1, bass.ds(e, 1), :].rearrange("p a d -> p (a d)"),
                       start=False, stop=True).then_inc(mm_ps, 1)

                def step(k):
                    for m, stage in ((k, turn_y), (k.back(1), expert)):
                        if m.valid(TILES):
                            stage(m)

                run(pe, step, 0, TILES + 1, 12, TILES - 6, 6)


def kernel(**inputs):
    import numpy as np
    import concourse.bacc as bacc
    from concourse.bass_utils import run_bass_kernel_spmd

    a = {k: np.asarray(v) for k, v in inputs.items()}

    def blocks(w, width):
        t = w.T.reshape(-1, 128, width)
        return np.ascontiguousarray(t.transpose(1, 0, 2).reshape(128, -1))

    def cols(v):
        return np.ascontiguousarray(v.reshape(-1, 128).T)

    x = a["x"].reshape(L, 3, 14, 16, 14, 16).transpose(0, 1, 2, 4, 3, 5).reshape(NG, G, KT, P)
    arrays = {
        "xt": np.ascontiguousarray(x.transpose(0, 3, 2, 1).reshape(NG, P, KT * G)),
        "w_tok": blocks(a["L0_tok_W"], D), "b_tok": a["L0_tok_b"],
        "log_a": cols(a["L0_attn_log_A"]), "w_b": blocks(a["L0_attn_W_B"], D), "b_b": cols(a["L0_attn_b_B"]),
        "w_c": blocks(a["L0_attn_W_C"], D), "b_c": a["L0_attn_b_C"],
        "w_d": blocks(a["L0_attn_W_D"], D), "b_d": a["L0_attn_b_D"], "log_dt": a["L0_attn_log_dt"],
        "w_in": blocks(a["L0_ffn_in_proj_w"], 3 * D), "b_qk": cols(a["L0_ffn_in_proj_b"][:2 * D]),
        "b_v": cols(a["L0_ffn_in_proj_b"][2 * D:]),
        "w_o": blocks(a["L0_ffn_out_proj_w"], D), "b_o": a["L0_ffn_out_proj_b"],
        "g1": a["L0_ffn_ln1_g"], "be1": a["L0_ffn_ln1_b"], "g2": a["L0_ffn_ln2_g"], "be2": a["L0_ffn_ln2_b"],
        "wg": np.ascontiguousarray(a["L0_ffn_wg"].reshape(FT, P, NE).transpose(1, 0, 2).reshape(P, FT * NE)),
        "w1t": np.ascontiguousarray(a["L0_ffn_w1"].transpose(0, 2, 1).reshape(NE, FK, P, D)
                                    .transpose(0, 2, 1, 3).reshape(NE, P, FK * D)),
        "w2": np.concatenate([a["L0_ffn_w2"].reshape(NE, FK, P, D).transpose(0, 2, 1, 3).reshape(NE, P, FK * D),
                              a["L0_ffn_b1"].reshape(NE, FK, P).transpose(0, 2, 1)], axis=2),
        "b2c": a["L0_ffn_b2"].reshape(1, NE, D),
    }
    nc = bacc.Bacc("TRN2", target_bir_lowering=False, num_devices=1)
    given = {}
    for name, v in arrays.items():
        arrays[name] = np.ascontiguousarray(v)
        given[name] = nc.dram_tensor(name, v.shape, mybir.dt.from_np(v.dtype), kind="ExternalInput").ap()
    out = nc.dram_tensor("out", (S, D), F32, kind="ExternalOutput").ap()
    build(nc, out=out, **given)
    r = run_bass_kernel_spmd(nc, [arrays], core_ids=[0])
    return r.results[0]["out"].reshape(L, N, D)
```
